# Optimizing a Trainium2 kernel written in Bass

```python
import numpy as np
import jax
import jax.numpy as jnp

def _softmax(x, axis=-1):
    return jax.nn.softmax(x, axis=axis)

def _gelu(x):
    return jax.nn.gelu(x, approximate=True)

def _silu(x):
    return jax.nn.silu(x)

def _sigmoid(x):
    return jax.nn.sigmoid(x)

def _layernorm(x, axis=-1, eps=1e-05):
    m = jnp.mean(x, axis=axis, keepdims=True)
    v = jnp.var(x, axis=axis, keepdims=True)
    return (x - m) / jnp.sqrt(v + eps)

def _scatter_add(tgt, idx, src, axis=0):
    return tgt.at[idx].add(src)

def _segment_sum(src, seg, n):
    return jax.ops.segment_sum(src, seg, n)
kernel_name = 'mk_adj_resnorm_d1_adj_r2_cad4e9'

def setup_inputs(seed: int=0):
    np.random.seed(seed)
    _w = jnp.asarray

    def _rec_inputs():
        import jax
        import jax.numpy as jnp
        _gk = jax.random.key(seed)
        x = -0.0002928 + 1 * jax.random.normal(jax.random.fold_in(_gk, 1), (4096, 256), jnp.float32)
        _a = jax.random.bernoulli(jax.random.fold_in(_gk, 2), 0.000488281, (4096, 4096))
        _af = _a.astype(jnp.float32)
        adj = _af
        return (x, adj)
    x, adj = _rec_inputs()

    def _L0_gnn_setup():
        import jax, jax.numpy as jnp
        import numpy as np
        SIZE_U = 2048
        SIZE_V = 2048
        N = SIZE_U + SIZE_V
        C_IN = 256
        C_OUT = 256
        EDGE_P = 0.005
        LEAKY_SLOPE = 0.01

        def _xavier_uniform(key, shape):
            fan_in, fan_out = shape
            lim = float(np.sqrt(6.0 / (fan_in + fan_out)))
            return jax.random.uniform(key, shape, jnp.float32, minval=-lim, maxval=lim)
        key = jax.random.key(seed)
        k1, k2, k3, k4 = jax.random.split(key, 4)
        x = jax.random.normal(k1, (N, C_IN), jnp.float32)
        adj = (jax.random.uniform(k2, (N, N)) < EDGE_P).astype(jnp.float32)
        weightr = _xavier_uniform(k3, (C_IN, C_OUT))
        weightd = _xavier_uniform(k4, (C_IN, C_OUT))
        bias = jnp.zeros((C_OUT,), jnp.float32)
        return {'x': x, 'adj': adj, 'weightr': weightr, 'weightd': weightd, 'bias': bias}
    _L0_gnn_all = _L0_gnn_setup()
    _L0_gnn_in = {k: v for k, v in _L0_gnn_all.items() if k in ('weightr', 'weightd', 'bias')}
    del _L0_gnn_all
    return {'x': x, 'adj': adj, 'L0_gnn_weightr': _L0_gnn_in['weightr'], 'L0_gnn_weightd': _L0_gnn_in['weightd'], 'L0_gnn_bias': _L0_gnn_in['bias']}

def reference(x, adj, L0_gnn_weightr, L0_gnn_weightd, L0_gnn_bias):
    import jax
    import jax.numpy as jnp

    def _L0_gnn_ref(x, adj, weightr, weightd, bias):
        import jax, jax.numpy as jnp
        import numpy as np
        SIZE_U = 2048
        SIZE_V = 2048
        N = SIZE_U + SIZE_V
        C_IN = 256
        C_OUT = 256
        EDGE_P = 0.005
        LEAKY_SLOPE = 0.01

        def _xavier_uniform(key, shape):
            fan_in, fan_out = shape
            lim = float(np.sqrt(6.0 / (fan_in + fan_out)))
            return jax.random.uniform(key, shape, jnp.float32, minval=-lim, maxval=lim)
        A = adj + jnp.eye(N, dtype=adj.dtype)
        deg = A.sum(axis=1)
        dinv = jnp.where(deg > 0, jax.lax.rsqrt(deg), 0.0)
        A = A * dinv[:, None] * dinv[None, :]
        R = x[:SIZE_U] @ weightr
        D = x[SIZE_U:] @ weightd
        h = jnp.concatenate([R, D], axis=0)
        out = A @ h + bias
        return jax.nn.leaky_relu(out, negative_slope=LEAKY_SLOPE)
    x = _layernorm(x + _L0_gnn_ref(x, adj, L0_gnn_weightr, L0_gnn_weightd, L0_gnn_bias), axis=-1)
    return x

_drawn_inputs = setup_inputs


def setup_inputs(seed=0):
    import zlib

    import numpy as np

    out = dict(_drawn_inputs(seed))
    spreads = {'L0_gnn_bias': (0.0, 0.1)}
    factors = {}
    for name, (base, spread) in spreads.items():
        noise = np.random.default_rng([zlib.crc32(name.encode()), seed]).standard_normal(out[name].shape)
        drawn = base * np.exp(spread * noise) if base else spread * noise
        out[name] = jnp.asarray(drawn.astype(out[name].dtype))
    for name, factor in factors.items():
        out[name] = (out[name] * factor).astype(out[name].dtype)
    return out
```

```python
import concourse.bass as bass
from concourse import mybir
from contextlib import ExitStack

N = 4096
C = 256
P = 128
TILES = N // P
HALF = TILES // 2
KC = C // P
GROUP = 4
GROUPS = TILES // GROUP
SLOPE = 0.01
EPS = 1e-5


def dense_path(nc, ctx, x, adj, wr, wd, bias, out):
    f32 = mybir.dt.float32
    ALU = mybir.AluOpType
    ACT = mybir.ActivationFunctionType
    AX = mybir.AxisListType

    def sb(name, shape):
        return ctx.enter_context(nc.sbuf_tensor("g_" + name, shape, f32))

    def pb(name, shape):
        return ctx.enter_context(nc.psum_tensor("g_" + name, shape, f32))

    def sem(name):
        return ctx.enter_context(nc.semaphore("g_" + name))

    adj_rows = [sb(f"adj_rows{u}", [P, N]) for u in range(2)]
    x_rows = [sb(f"x_rows{u}", [P, C]) for u in range(2)]
    x_cols = [sb(f"x_cols{u}", [P, KC * P]) for u in range(2)]
    adj_cols = [sb(f"adj_cols{u}", [P, GROUP * P]) for u in range(2)]
    weights = sb("weights", [P, 2, KC, C])
    feats = sb("feats", [P, TILES, C])
    bias_rows = sb("bias_rows", [P, C])
    ident = sb("ident", [P, P])
    deg = sb("deg", [P, 4])
    dinv = sb("dinv", [P, TILES])
    minus_half = sb("minus_half", [P, 1])
    z = sb("z", [P, 4, C])
    stats = sb("stats", [P, 16])
    y = [sb(f"y{u}", [P, C]) for u in range(2)]
    cols_ps = [pb(f"cols_ps{u}", [P, GROUP * P]) for u in range(2)]
    prod_ps = [pb(f"prod_ps{u}", [P, C]) for u in range(2)]

    const_ld = sem("const_ld")
    ident_ok = sem("ident_ok")
    a_ld = [sem(f"a_ld{u}") for u in range(2)]
    a_xT_ps = sem("a_xT_ps")
    a_xT = sem("a_xT")
    a_prod = sem("a_prod")
    a_deg = sem("a_deg")
    a_pow = sem("a_pow")
    a_feat = sem("a_feat")
    dve_step = sem("dve_step")
    b_ld = [sem(f"b_ld{u}") for u in range(2)]
    b_T_ps = sem("b_T_ps")
    b_T = sem("b_T")
    b_prod = sem("b_prod")
    b_read = sem("b_read")
    b_var = sem("b_var")
    b_rstd = sem("b_rstd")
    b_y = sem("b_y")
    b_st = [sem(f"b_st{u}") for u in range(2)]

    LINKS_A = 3
    LINKS_B = 6

    with nc.Block() as block:

        @block.sync
        def _(sp):
            for s, w in enumerate((wr, wd)):
                sp.dma_start(weights[:, s], w.rearrange("(k p) n -> p k n", p=P)).then_inc(const_ld, 16)
            sp.dma_start(bias_rows[:, :], bias.partition_broadcast(P)).then_inc(const_ld, 16)
            def load(rows, ld):
                for u, r in enumerate(rows):
                    sp.dma_start(x_rows[u][:, :], x[bass.ds(r * P, P), :]).then_inc(ld[u], 16)
                    sp.dma_start(adj_rows[u][:, :], adj[bass.ds(r * P, P), :]).then_inc(ld[u], 16)

            load((0, 1), a_ld)
            with sp.Fori(1, TILES // 2) as pair:
                i = pair * 2
                sp.wait_ge(a_feat, i)
                load((i, i + 1), a_ld)
            sp.wait_ge(a_feat, TILES)
            load((0, 1), b_ld)
            with sp.Fori(1, TILES // 2) as pair:
                i = pair * 2
                sp.wait_ge(b_read, i)
                load((i, i + 1), b_ld)

        @block.scalar
        def _(act):
            with act.Fori(0, TILES // 2) as pair:
                i = pair * 2
                for u in range(2):
                    act.wait_ge(a_xT_ps, i + u + 1)
                    nc.scalar.copy(x_cols[u][:, :], cols_ps[u][:, 0:KC * P]).then_inc(a_xT, 1)
            with act.Fori(0, TILES // 2) as pair:
                i = pair * 2
                for u in range(2):
                    for g in range(GROUPS):
                        act.wait_ge(b_T_ps, (i + u) * GROUPS + g + 1)
                        nc.scalar.copy(adj_cols[g % 2][:, :], cols_ps[g % 2][:, :]).then_inc(b_T, 1)

        @block.tensor
        def _(pe):
            pe.wait_ge(ident_ok, 3)
            pe.wait_ge(const_ld, 48)
            for s in range(2):
                with pe.Fori(s * HALF // 2, (s + 1) * HALF // 2) as pair:
                    i = pair * 2
                    for u in range(2):
                        pe.wait_ge(a_ld[u], i * 16 + 32)
                        for k in range(KC):
                            t = nc.tensor.transpose(cols_ps[u][:, k * P:(k + 1) * P],
                                                    x_rows[u][:, k * P:(k + 1) * P], ident[:, :])
                        t.then_inc(a_xT_ps, 1)
                        pe.wait_ge(a_xT, i + u + 1)
                        for k in range(KC):
                            m = nc.tensor.matmul(prod_ps[u][:, :], x_cols[u][:, k * P:(k + 1) * P],
                                                 weights[:, s, k, :], start=(k == 0), stop=(k == KC - 1))
                        m.then_inc(a_prod, 1)
            pe.wait_ge(a_feat, TILES)

            def transposes(u, g):
                for j in range(GROUP):
                    c = g * GROUP + j
                    t = nc.tensor.transpose(cols_ps[g % 2][:, j * P:(j + 1) * P],
                                            adj_rows[u][:, c * P:(c + 1) * P], ident[:, :])
                t.then_inc(b_T_ps, 1)

            with pe.Fori(0, TILES // 2) as pair:
                i = pair * 2
                for u in range(2):
                    pe.wait_ge(b_ld[u], i * 16 + 32)
                    transposes(u, 0)
                    for g in range(GROUPS):
                        if g + 1 < GROUPS:
                            transposes(u, g + 1)
                        pe.wait_ge(b_T, (i + u) * GROUPS + g + 1)
                        for j in range(GROUP):
                            c = g * GROUP + j
                            m = nc.tensor.matmul(prod_ps[u][:, :], adj_cols[g % 2][:, j * P:(j + 1) * P],
                                                 feats[:, c, :], start=(c == 0), stop=(c == TILES - 1))
                    m.then_inc(b_prod, 1)

        @block.gpsimd
        def _(pool):
            nc.gpsimd.memset(minus_half[:, :], -0.5).then_inc(ident_ok, 1)
            nc.gpsimd.memset(ident[:, :], 0.0).then_inc(ident_ok, 1)
            pool.wait_ge(ident_ok, 2)
            nc.gpsimd.affine_select(out=ident[:, :], in_=ident[:, :], compare_op=ALU.not_equal, fill=1.0, base=0,
                                    pattern=[[-1, P]], channel_multiplier=1).then_inc(ident_ok, 1)
            with pool.Fori(0, TILES // 2) as pair:
                i = pair * 2
                for u in range(2):
                    pool.wait_ge(a_deg, i + u + 1)
                    nc.gpsimd.tensor_tensor(deg[:, 2:3], deg[:, 1:2], minus_half[:, :], ALU.pow).then_inc(a_pow, 1)
            with pool.Fori(0, TILES // 2) as pair:
                i = pair * 2
                for u in range(2):
                    pool.wait_ge(b_var, i + u + 1)
                    nc.gpsimd.tensor_tensor(stats[:, 13:14], stats[:, 12:13], minus_half[:, :],
                                            ALU.pow).then_inc(b_rstd, 1)
                    pool.wait_ge(b_y, i + u + 1)
                    pool.dma_start(out[bass.ds((i + u) * P, P), :], y[u][:, :]).then_inc(b_st[u], 16)
                for u in range(2):
                    pool.wait_ge(b_st[u], i * 8 + 16)

        @block.vector
        def _(dve):
            with dve.Fori(0, TILES // 2) as pair:
                i = pair * 2
                for u in range(2):
                    t = i + u
                    links = [t * LINKS_A]

                    def link(ins):
                        ins.then_inc(dve_step, 1)
                        links[0] = links[0] + 1
                        dve.wait_ge(dve_step, links[0])

                    dve.wait_ge(a_ld[u], i * 16 + 32)
                    link(nc.vector.reduce_sum(deg[:, 0:1], adj_rows[u][:, :], axis=AX.X))
                    nc.vector.tensor_scalar(deg[:, 1:2], deg[:, 0:1], 1.0, 1e-38, ALU.add, ALU.max).then_inc(a_deg, 1)
                    link(nc.vector.tensor_scalar(deg[:, 3:4], deg[:, 0:1], 1.0, 0.0, ALU.add, ALU.is_gt))
                    dve.wait_ge(a_pow, t + 1)
                    link(nc.vector.tensor_tensor(dinv[:, bass.ds(t, 1)], deg[:, 2:3], deg[:, 3:4], ALU.mult))
                    dve.wait_ge(a_prod, t + 1)
                    nc.vector.tensor_scalar(feats[:, bass.ds(t, 1), :], prod_ps[u][:, :], dinv[:, bass.ds(t, 1)],
                                            None, ALU.mult).then_inc(a_feat, 1)
            dve.wait_ge(const_ld, 48)
            with dve.Fori(0, TILES // 2) as pair:
                i = pair * 2
                for u in range(2):
                    t = i + u
                    links = [t * LINKS_B + TILES * LINKS_A]

                    def link(ins):
                        ins.then_inc(dve_step, 1)
                        links[0] = links[0] + 1
                        dve.wait_ge(dve_step, links[0])

                    dve.wait_ge(b_prod, t + 1)
                    link(nc.vector.tensor_tensor(z[:, 0, :], prod_ps[u][:, :], feats[:, bass.ds(t, 1), :], ALU.add))
                    link(nc.vector.scalar_tensor_tensor(z[:, 1, :], z[:, 0, :], dinv[:, bass.ds(t, 1)],
                                                        bias_rows[:, :], ALU.mult, ALU.add))
                    link(nc.vector.scalar_tensor_tensor(z[:, 2, :], z[:, 1, :], SLOPE, z[:, 1, :], ALU.mult, ALU.max))
                    dve.wait_ge(b_ld[u], i * 16 + 32)
                    nc.vector.tensor_tensor(z[:, 3, :], z[:, 2, :], x_rows[u][:, :], ALU.add).then_inc(b_read, 1)
                    dve.wait_ge(b_read, t + 1)
                    link(nc.vector.bn_stats(stats[:, 0:6], z[:, 3, :]))
                    nc.vector.tensor_tensor(stats[:, 6:8], stats[:, 1:3], stats[:, 4:6], ALU.add)
                    link(nc.vector.tensor_tensor(stats[:, 8:9], stats[:, 1:2], stats[:, 4:5], ALU.subtract))
                    nc.vector.tensor_scalar(stats[:, 9:10], stats[:, 6:7], 0.5, None, ALU.mult)
                    nc.vector.tensor_scalar(stats[:, 11:12], stats[:, 7:8], 1.0 / C, EPS, ALU.mult, ALU.add)
                    link(nc.vector.tensor_tensor(stats[:, 10:11], stats[:, 8:9], stats[:, 8:9], ALU.mult))
                    nc.vector.scalar_tensor_tensor(stats[:, 12:13], stats[:, 10:11], 0.25, stats[:, 11:12],
                                                   ALU.mult, ALU.add).then_inc(b_var, 1)
                    dve.wait_ge(b_rstd, t + 1)
                    nc.vector.tensor_scalar(y[u][:, :], z[:, 3, :], stats[:, 9:10], stats[:, 13:14],
                                            ALU.subtract, ALU.mult).then_inc(b_y, 1)


def program(nc, x, adj, wr, wd, bias, out):
    with ExitStack() as ctx:
        dense_path(nc, ctx, x, adj, wr, wd, bias, out)


_INS = ['x', 'adj', 'L0_gnn_weightr', 'L0_gnn_weightd', 'L0_gnn_bias']


def kernel(**inputs):
    import numpy as _np
    import concourse.bacc as _bacc
    from concourse import mybir as _mybir
    from concourse.bass_utils import run_bass_kernel_spmd as _run

    nc = _bacc.Bacc("TRN2", target_bir_lowering=False, num_devices=1)
    arrays, args = {}, []
    for name in _INS:
        a = _np.ascontiguousarray(inputs[name])
        arrays[f"in_{name}_dram"] = a
        args.append(nc.dram_tensor(f"in_{name}_dram", a.shape, _mybir.dt.from_np(a.dtype), kind="ExternalInput").ap())
    args.append(nc.dram_tensor("out_0_dram", (N, C), _mybir.dt.float32, kind="ExternalOutput").ap())
    program(nc, *args)
    r = _run(nc, [arrays], core_ids=[0])
    return r.results[0]["out_0_dram"]
```

```python
import concourse.bass as bass
from concourse import mybir
from contextlib import ExitStack

N = 4096
C = 256
P = 128
TILES = N // P
HALF = TILES // 2
KC = C // P
GROUP = 4
GROUPS = TILES // GROUP
SLOPE = 0.01
EPS = 1e-5

Q = 4
LANES = P // Q
SIDES = 2
PAIRS = HALF // 2
SB = 8
NSB = TILES // SB
UNIT = SB * P
PARTS = 2
BANK = 512
MANTISSA = 23
TOP = 14
DEG_MAX = float(N + 1)


def tile_rows(c):
    return c // HALF, c % HALF // 2, c % 2


def split_path(nc, ctx, x, adj, wr, wd, bias, out, flag):
    f32 = mybir.dt.float32
    f16 = mybir.dt.float16
    bf16 = mybir.dt.bfloat16
    u32 = mybir.dt.uint32
    i32 = mybir.dt.int32
    u16 = mybir.dt.uint16
    ALU = mybir.AluOpType
    ACT = mybir.ActivationFunctionType
    AX = mybir.AxisListType
    RMAX = bass.bass_isa.ReduceOp.max

    def sb(name, shape, dt=f32):
        return ctx.enter_context(nc.sbuf_tensor("s_" + name, shape, dt))

    def sem(name):
        return ctx.enter_context(nc.semaphore("s_" + name))

    feats = sb("feats", [P, TILES + 1, C])
    raw = sb("raw", [P, 4, 2 * N // Q])
    conv = sb("conv", [P, 2, 2, 2, N // Q], bf16)
    store = sb("store", [P, 62, UNIT], bf16)
    HELD = {(0, 1): 0, (2, 3): 0, (0, 3): 8, (0, 2): 16, (1, 2): 24, (1, 3): 32}
    DIAG = 40
    RING = {1: (48, 6), 2: (48, 3), 3: (16, 5)}
    SUMS = {0: 54, 1: 58, 2: 50}
    x_early = store[:, 24:40, :].rearrange("p a b -> p (a b)").bitcast(f32).rearrange("p (c n) -> p c n", n=C)
    x_cols = store[:, 48:52, :].bitcast(f32)
    ident32 = store[:, 52, 0:2 * P].bitcast(f32)
    weights = store[:, 54:56, :].rearrange("p a b -> p (a b)").bitcast(f32).rearrange(
        "p (s k n) -> p s k n", s=2, k=KC)
    stats = store[:, 48, :].bitcast(f32)
    x_late = raw[:, :, :].rearrange("p a b -> p (a b)").rearrange("p (c n) -> p c n", n=C)
    z_bufs, y_bufs = (conv[:, h].rearrange("p a r w -> p (a r w)").bitcast(f32).rearrange("p (b n) -> p b n", b=4)
                      for h in range(2))

    GRANULES = TILES // 2 * Q

    def by_dve(n):
        return n % 2 == 1

    N_DVE = sum(by_dve(n) for n in range(GRANULES))
    bias_rows = sb("bias_rows", [P, C])
    same_lane = sb("same_lane", [P, P])
    ident16 = sb("ident16", [P, P], f16)
    row_parts = sb("row_parts", [P, 4, Q])
    own_quad = sb("own_quad", [P, Q])
    degs = sb("degs", [P, TILES])
    small = sb("small", [P, 16])
    good = sb("good", [P, TILES])
    dinv = sb("dinv", [P, TILES])
    up = sb("up", [P, 2])
    down = sb("down", [P, TILES])
    low_bits = sb("low_bits", [P, GRANULES])
    hmax = sb("hmax", [P, TILES // 2])
    own_max, gmax, scale, unscale, ebits, bad, bad_all = (small[:, k:k + 1] for k in range(7))
    half_neg = small[:, 8:10]
    quad_sums = small[:, 12:16]

    banks = [ctx.enter_context(nc.psum_tensor(f"s_bank{k}", [P, BANK], f32)) for k in range(8)]
    COL_BANKS = banks[4:7]
    deg_bank = banks[7]

    w_ld = sem("w_ld")
    x_ld = sem("x_ld")
    xl_ld = sem("xl_ld")
    raw_ld = [sem(f"raw_ld{k}") for k in range(4)]
    consts = sem("consts")
    consts_v = sem("consts_v")
    xT_ps, xT_ok = sem("xT_ps"), sem("xT_ok")
    h_ps, h_ok = sem("h_ps"), sem("h_ok")
    hmax_ok, gmax_ok, scale_ok = sem("hmax_ok"), sem("gmax_ok"), sem("scale_ok")
    conv_ok = sem("conv_ok")
    chk_act = sem("chk_act")
    chk_dve = sem("chk_dve")
    turned = sem("turned")
    deg_ps = sem("deg_ps")
    deg_ok = sem("deg_ok")
    pow_ok = sem("pow_ok")
    up_ok = sem("up_ok")
    parts_ok = sem("parts_ok")
    step_done = sem("step_done")
    sums_ok = sem("sums_ok")
    col_ps = sem("col_ps")
    col_end = sem("col_end")
    link = sem("link")
    z_ok, act_ok, res_ok = sem("z_ok"), sem("act_ok"), sem("res_ok")
    var_ok, rstd_ok, shift_ok, y_ok = sem("var_ok"), sem("rstd_ok"), sem("shift_ok"), sem("y_ok")
    stored = [sem(f"stored{k}") for k in range(4)]
    bad_ok, bad_all_ok, flag_ok = sem("bad_ok"), sem("bad_all_ok"), sem("flag_ok")

    N_CONSTS = 3 + 2 * Q - 1

    def degs_cl(c):
        return small[:, 10 + c % 2:11 + c % 2]

    def unit(c, J):
        I, e = divmod(c, SB)
        if J > I:
            return HELD[I, J] + e
        if J == I:
            return DIAG + e
        first, depth = RING[I]
        return first + e % depth * I + J

    def chunk(c, t):
        return store[:, unit(c, t // SB), :].rearrange("p (g m r) -> p g m r", m=P, r=2)[:, t % SB // 2, :, t % 2]

    def part(t, k):
        return feats[:, t, :].bitcast(f16)[:, k * C:(k + 1) * C]

    def sums(I, b):
        return store[:, SUMS[I] + b, :].bitcast(f32)

    def low(n, part=slice(None)):
        return raw[:, n % 4, part].bitcast(u16).rearrange("p (n t) -> p n t", t=2)[:, :, 0]

    def looks(n):
        k = sum(by_dve(m) for m in range(n + 1))
        return (chk_dve, k) if by_dve(n) else (chk_act, n + 1 - k)

    def stat(k, n, m=1):
        return stats[:, k % 4 * 24 + n:k % 4 * 24 + n + m]

    COLS = [(I, J, b) for J in range(1, NSB) for I in range(J) for b in range(SB // 2)]
    LAST = NSB - 1
    TAKES = []
    for I in range(LAST):
        TAKES += [("row", I, b) for b in range(SB // 2)]
        TAKES += [("col", k, b) for k, (_, J, b) in enumerate(COLS) if J == I]

    def taken(kind, n, b):
        return TAKES.index((kind, n, b)) + 1

    def sums_written(I, b):
        return max(n + 1 for n, (kind, k, b2) in enumerate(TAKES)
                   if b2 == b and (k if kind == "row" else COLS[k][0]) == I)
    ENDS = [("row", b) for b in range(SB // 2)]
    for k, (I, J, b) in enumerate(COLS):
        if J == LAST:
            ENDS.append(("col", k))
    first_col = next(k for k, (I, J, b) in enumerate(COLS) if J == LAST)
    ENDS = [ENDS[k] for k in (0, 1, 4, 2, 5, 3)] + ENDS[6:]

    def end_tile(kind, k):
        return LAST * SB + 2 * k if kind == "row" else COLS[k][0] * SB + 2 * COLS[k][2]

    with nc.Block() as block:

        @block.sync
        def _(sp):
            for s, w in enumerate((wr, wd)):
                sp.dma_start(weights[:, s], w.rearrange("(k p) n -> p k n", p=P)).then_inc(w_ld, 16)
            sp.dma_start(bias_rows[:, :], bias.partition_broadcast(P)).then_inc(w_ld, 16)
            x_v = x.rearrange("(s q g j r) n -> s q j g (r n)", s=SIDES, q=Q, g=PAIRS, j=LANES, r=2)

            def load_x(dst, ld):
                for side in range(SIDES):
                    for q in range(Q):
                        sp.dma_start(dst[q * LANES:(q + 1) * LANES, side * HALF:(side + 1) * HALF, :].rearrange(
                            "p (g r) n -> p g (r n)", r=2), x_v[side, q]).then_inc(ld, 16)

            load_x(x_early, x_ld)
            adj_v = adj.rearrange("(s a g u r) (t q w) -> s g a q u (r t) w", s=SIDES, a=Q, g=PAIRS, u=LANES, r=2,
                                  t=SIDES, q=Q)
            for n in range(GRANULES):
                pair, a = divmod(n, Q)
                if n >= 4:
                    sp.wait_ge(conv_ok, n - 3)
                    sp.wait_ge(*looks(n - 4))
                for q in range(Q):
                    sp.dma_start(raw[q * LANES:(q + 1) * LANES, n % 4, :].rearrange("p (m w) -> p m w", m=2 * SIDES),
                                 adj_v[pair // PAIRS, pair % PAIRS, a, q]).then_inc(raw_ld[n % 4], 16)
            sp.wait_ge(conv_ok, GRANULES)
            sp.wait_ge(chk_act, GRANULES - N_DVE)
            sp.wait_ge(chk_dve, N_DVE)
            load_x(x_late, xl_ld)
            out_v = out.rearrange("(s q g j r) n -> s g q j (r n)", s=SIDES, q=Q, g=PAIRS, j=LANES, r=2)
            for k, end in enumerate(ENDS):
                s, g, _r = tile_rows(end_tile(*end))
                sp.wait_ge(y_ok, k + 1)
                for q in range(Q):
                    sp.dma_start(out_v[s, g, q], y_bufs[q * LANES:(q + 1) * LANES, k % 4, :]).then_inc(
                        stored[k % 4], 16)
            for k in range(4):
                sp.wait_ge(stored[k], 16 * Q * len(ENDS) // 4)

        @block.scalar
        def _(act):
            def look(n):
                act.wait_ge(conv_ok, n + 1)
                nc.scalar.activation(low(n), low(n), ACT.Copy, accum_out=low_bits[:, n:n + 1]).then_inc(chk_act, 1)

            for n in range(GRANULES):
                pair, a = divmod(n, Q)
                act.wait_ge(raw_ld[n % 4], 16 * Q * (pair + 1))
                if n % 2 == 0 and n >= 4:
                    act.wait_ge(turned, n // 2 - 1)
                if a == 0 and pair >= 2:
                    act.wait_ge(deg_ps, 2 * pair - 2)
                for r in range(2):
                    i = nc.scalar.activation(conv[:, n // 2 % 2, a % 2, r, :],
                                             raw[:, n % 4, r * N // Q:(r + 1) * N // Q], ACT.Copy,
                                             accum_out=row_parts[:, (2 * pair + r) % 4, a:a + 1])
                i.then_inc(conv_ok, 1)
                if n >= 1 and not by_dve(n - 1):
                    look(n - 1)
            if not by_dve(GRANULES - 1):
                look(GRANULES - 1)

            def finish(k):
                act.wait_ge(shift_ok, k + 1)
                for v in range(2):
                    i = nc.scalar.activation(y_bufs[:, k % 4, v * C:(v + 1) * C], z_bufs[:, k % 4, v * C:(v + 1) * C],
                                             ACT.Identity, bias=stat(k, 20 + v), scale=stat(k, 18 + v))
                i.then_inc(y_ok, 1)

            for k in range(len(ENDS)):
                if k >= 4:
                    act.wait_ge(stored[k % 4], 16 * Q * (k // 4))
                finish(k)

        @block.tensor
        def _(pe):
            def turn_x(b):
                if b >= 2:
                    pe.wait_ge(xT_ok, b - 1)
                for v in range(2):
                    for k in range(KC):
                        i = nc.tensor.transpose(banks[4 + b % 2][:, (v * KC + k) * P:(v * KC + k + 1) * P],
                                                x_early[:, 2 * b + v, k * P:(k + 1) * P], ident32)
                i.then_inc(xT_ps, 1)

            pe.wait_ge(consts, 2)
            pe.wait_ge(w_ld, 48)
            pe.wait_ge(x_ld, 16 * SIDES * Q)
            turn_x(0)
            for b in range(TILES // 2):
                if b + 1 < TILES // 2:
                    turn_x(b + 1)
                pe.wait_ge(xT_ok, b + 1)
                if b >= 2:
                    pe.wait_ge(h_ok, b - 1)
                for v in range(2):
                    for k in range(KC):
                        i = nc.tensor.matmul(banks[(6, 3)[b % 2]][:, v * C:(v + 1) * C],
                                             x_cols[:, b % 4, (v * KC + k) * P:(v * KC + k + 1) * P],
                                             weights[:, b // (HALF // 2), k, :], start=(k == 0), stop=(k == KC - 1))
                i.then_inc(h_ps, 1)

            pe.wait_ge(consts, N_CONSTS)
            k_col = 0
            for c in range(TILES):
                I, e = divmod(c, SB)
                pe.wait_ge(conv_ok, Q * (c // 2 + 1))
                if c >= 1:
                    pe.wait_ge(deg_ok, c)
                nc.tensor.matmul(deg_bank[:, c * Q:(c + 1) * Q], same_lane[:, :], row_parts[:, c % 4, :],
                                 start=True, stop=True).then_inc(deg_ps, 1)

                opened = e % 2 == 1

                def multiply(row, t, last):
                    nonlocal opened
                    for k in range(PARTS):
                        i = nc.tensor.matmul(banks[row % SB // 2][:, row % 2 * C:(row % 2 + 1) * C],
                                             chunk(row, t), part(t, k),
                                             start=not opened, stop=last and k == PARTS - 1, skip_group_check=True)
                        opened = True
                    return i

                pe.wait_ge(turned, 2 * (c // 2 + 1))
                if e % 2 == 0 and I >= 1:
                    pe.wait_ge(sums_ok, taken("row", I - 1, e // 2))
                for t in range(c):
                    multiply(c, t, False)
                pe.wait_ge(parts_ok, c + 1)
                multiply(c, c, False)
                for k in range(PARTS):
                    i = nc.tensor.matmul(banks[e // 2][:, e % 2 * C:(e % 2 + 1) * C], ident16[:, :], part(c, k),
                                         start=False, stop=e == SB - 1 and k == PARTS - 1, skip_group_check=True)
                for row in range(I * SB, c):
                    i = multiply(row, c, e == SB - 1)
                i.then_inc(step_done, 1)

                while e == SB - 1 and k_col < len(COLS) and COLS[k_col][1] == I:
                    I2, J, b = COLS[k_col]
                    if k_col >= 3 and COLS[k_col - 3][1] < LAST:
                        pe.wait_ge(sums_ok, taken("col", k_col - 3, COLS[k_col - 3][2]))
                    elif k_col >= 3:
                        pe.wait_ge(col_end, k_col - 3 - first_col + 1)
                    for v in range(2):
                        row = I2 * SB + 2 * b + v
                        for t in range(J * SB, (J + 1) * SB):
                            for k in range(PARTS):
                                i = nc.tensor.matmul(COL_BANKS[k_col % 3][:, v * C:(v + 1) * C], chunk(row, t),
                                                     part(t, k), start=(v == 0 and t == J * SB and k == 0),
                                                     stop=(t == (J + 1) * SB - 1 and k == PARTS - 1),
                                                     skip_group_check=True)
                    i.then_inc(col_ps, 1)
                    k_col += 1

        @block.gpsimd
        def _(pool):
            nc.gpsimd.memset(ident32, 0.0)
            nc.gpsimd.memset(ident16[:, :], 0.0)
            nc.gpsimd.memset(half_neg, -0.5)
            nc.gpsimd.memset(same_lane[:, :], 0.0).then_inc(consts, 1)
            diagonals = [(ident32, 0), (ident16[:, :], 0)] + [(same_lane[:, :], d) for d in range(LANES - P, P, LANES)]
            for n, (m, d) in enumerate(diagonals):
                pool.wait_ge(consts, n + 1)
                nc.gpsimd.affine_select(out=m, in_=m, compare_op=ALU.not_equal, fill=1.0, base=-d,
                                        pattern=[[-1, P]], channel_multiplier=1).then_inc(consts, 1)
            pool.wait_ge(hmax_ok, 1)
            nc.gpsimd.partition_all_reduce(gmax, own_max, P, RMAX).then_inc(gmax_ok, 1)
            for c in range(TILES):
                pool.wait_ge(deg_ok, c + 1)
                nc.gpsimd.tensor_tensor(dinv[:, c:c + 1], degs_cl(c), half_neg[:, 0:1], ALU.pow).then_inc(pow_ok, 1)
                if c == 0:
                    pool.wait_ge(scale_ok, 1)
                if c >= 2:
                    pool.wait_ge(parts_ok, c - 1)
                pool.wait_ge(pow_ok, c + 1)
                nc.gpsimd.tensor_tensor(up[:, c % 2:c % 2 + 1], dinv[:, c:c + 1], scale, ALU.mult).then_inc(up_ok, 1)
            pool.wait_ge(bad_ok, 1)
            nc.gpsimd.partition_all_reduce(bad_all, bad, P, RMAX).then_inc(bad_all_ok, 1)
            for k in range(len(ENDS)):
                pool.wait_ge(var_ok, k + 1)
                nc.gpsimd.tensor_tensor(stat(k, 18, 2), stat(k, 16, 2), half_neg,
                                        ALU.pow).then_inc(rstd_ok, 1)
                pool.wait_ge(rstd_ok, k + 1)
                nc.gpsimd.tensor_tensor(stat(k, 20, 2), stat(k, 22, 2), stat(k, 18, 2), ALU.mult).then_inc(shift_ok, 1)

        @block.vector
        def _(dve):
            links = [0]

            def then(i):
                links[0] += 1
                i.then_inc(link, 1)
                dve.wait_ge(link, links[0])

            then(nc.vector.memset(own_quad[:, :], 0.0))
            for q in range(Q):
                i = nc.vector.memset(own_quad[q * LANES:(q + 1) * LANES, q:q + 1], 1.0)
            then(i)

            def turn(pair):
                for c in (2 * pair, 2 * pair + 1):
                    I, e = divmod(c, SB)
                    if I >= 1:
                        dve.wait_ge(step_done, I * SB)
                        if e >= RING[I][1]:
                            dve.wait_ge(step_done, c - RING[I][1] + 1)
                        if I > 1 and e < RING[I][1] or I == 2:
                            dve.wait_ge(col_ps, ready_after(c) + 1)
                for h in range(2):
                    dve.wait_ge(conv_ok, Q * pair + 2 * h + 2)
                    src = conv[:, h].rearrange("p a r w -> p (a r w)").bitcast(u32).rearrange(
                        "p (a r J m) -> p r J a m", a=2, r=2, J=NSB)
                    for r in range(2):
                        for J in range(NSB):
                            dst = store[:, unit(2 * pair + r, J), :].bitcast(u32).rearrange(
                                "p (g a u) -> p a g u", a=Q, u=LANES)[:, 2 * h:2 * h + 2]
                            i = nc.vector.transpose(dst, src[:, r, J].rearrange("p a (g u) -> p a g u", u=LANES))
                    i.then_inc(turned, 1)
                    for n in (Q * pair + 2 * h, Q * pair + 2 * h + 1):
                        if by_dve(n):
                            look(n)

            def look(n):
                first, second = (low(n, slice(v * N // Q, (v + 1) * N // Q)) for v in range(2))
                nc.vector.tensor_tensor_reduce(out=first, in0=first, in1=second, scale=1.0, scalar=0.0, op0=ALU.add,
                                               op1=ALU.max, accum_out=low_bits[:, n:n + 1]).then_inc(chk_dve, 1)

            def ready_after(c):
                I, e = divmod(c, SB)
                return {2: e // 2, 3: SB // 2 + (e * I + I - 1) // 2}[I]

            def degrees(c):
                dve.wait_ge(deg_ps, c + 1)
                then(nc.vector.tensor_tensor_reduce(out=quad_sums,
                                                    in0=deg_bank[:, c * Q:(c + 1) * Q],
                                                    in1=own_quad[:, :], scale=1.0, scalar=1.0, op0=ALU.mult,
                                                    op1=ALU.add, accum_out=degs[:, c:c + 1]))
                if c >= 2:
                    dve.wait_ge(up_ok, c - 1)
                nc.vector.tensor_scalar(degs_cl(c), degs[:, c:c + 1], 1.0, None, ALU.max).then_inc(deg_ok, 1)

            def make_parts(c):
                dve.wait_ge(up_ok, c + 1)
                f = up[:, c % 2:c % 2 + 1]
                then(nc.vector.tensor_scalar(part(c, 0), feats[:, c + 1, :], f, None, ALU.mult))
                nc.vector.scalar_tensor_tensor(part(c, 1), feats[:, c + 1, :], f, part(c, 0), ALU.mult,
                                               ALU.subtract).then_inc(parts_ok, 1)

            def keep_product(b):
                dve.wait_ge(h_ps, b + 1)
                nc.vector.tensor_copy(feats[:, 2 * b + 1:2 * b + 3, :],
                                      banks[(6, 3)[b % 2]][:, :].rearrange("p (v n) -> p v n", v=2)).then_inc(h_ok, 1)

            def largest(b):
                dve.wait_ge(h_ok, b + 1)
                return nc.vector.tensor_reduce(hmax[:, b:b + 1], feats[:, 2 * b + 1:2 * b + 3, :], AX.XY, ALU.max,
                                               apply_absolute_value=True)

            early = {7: 0, 13: 1}
            for b in range(TILES // 2):
                dve.wait_ge(xT_ps, b + 1)
                nc.vector.tensor_copy(x_cols[:, b % 4, :], banks[4 + b % 2][:, :]).then_inc(xT_ok, 1)
                if b >= 1:
                    keep_product(b - 1)
                if b >= 2:
                    largest(b - 2)
                if b in early:
                    turn(early[b])
            b = TILES // 2 - 1
            largest(b - 1)
            keep_product(b)
            then(largest(b))
            nc.vector.tensor_reduce(own_max, hmax[:, :], AX.X, ALU.max).then_inc(hmax_ok, 1)
            turned_to = len(early)
            dve.wait_ge(gmax_ok, 1)
            then(nc.vector.tensor_scalar(ebits, gmax, 2.0 ** -100, None, ALU.max))
            then(nc.vector.tensor_scalar(ebits.bitcast(i32), ebits.bitcast(i32), 0x7F800000, None, ALU.bitwise_and))
            nc.vector.tensor_scalar(unscale.bitcast(i32), ebits.bitcast(i32), float(-(TOP << MANTISSA)), None, ALU.add)
            nc.vector.tensor_scalar(scale.bitcast(i32), ebits.bitcast(i32), -1.0, float((254 + TOP) << MANTISSA),
                                    ALU.mult, ALU.add).then_inc(scale_ok, 1)

            def take(kind, n, b):
                if kind == "row":
                    i = nc.vector.tensor_copy(sums(n, b), banks[b][:, :])
                else:
                    I, J, _ = COLS[n]
                    dve.wait_ge(col_ps, n + 1)
                    dve.wait_ge(sums_ok, taken("row", J - 1, b) if I == J - 1 else taken("col", before[n], b))
                    i = nc.vector.tensor_tensor(sums(I, b), COL_BANKS[n % 3][:, :], sums(I, b), ALU.add)
                i.then_inc(sums_ok, 1)

            before = {n: max((m for m in range(n) if COLS[m][0] == COLS[n][0] and COLS[m][2] == COLS[n][2]), default=-1)
                      for n in range(len(COLS))}

            for c in range(TILES):
                I, e = divmod(c, SB)
                if turned_to <= c // 2:
                    turn(turned_to)
                    turned_to += 1
                degrees(c)
                make_parts(c)
                depth = RING[I][1] if I else SB
                if I >= 2 and turned_to < (I + 1) * SB // 2 and 2 * turned_to + 2 - min(depth, 4) <= c:
                    turn(turned_to)
                    turned_to += 1
                if e < SB - 1 or I == LAST:
                    continue
                dve.wait_ge(step_done, c + 1)
                for kind, n, b in TAKES:
                    if kind == "row" and n == I:
                        take(kind, n, b)
                    if kind == "col" and COLS[n][1] == I:
                        take(kind, n, b)
                        nxt = 2 * turned_to + 1
                        if nxt - c - 1 < RING[I + 1][1] and ready_after(nxt) <= n:
                            turn(turned_to)
                            turned_to += 1

            then(nc.vector.tensor_scalar(down[:, :], dinv[:, :], unscale, None, ALU.mult))
            dve.wait_ge(chk_act, GRANULES - N_DVE)
            dve.wait_ge(chk_dve, N_DVE)
            nc.vector.tensor_reduce(own_max, low_bits[:, :], AX.X, ALU.max)
            then(nc.vector.tensor_scalar(good[:, :], degs[:, :], 1.0, None, ALU.is_ge))
            then(nc.vector.scalar_tensor_tensor(good[:, :], degs[:, :], DEG_MAX, good[:, :], ALU.is_le, ALU.mult))
            then(nc.vector.tensor_reduce(ebits, good[:, :], AX.X, ALU.min))
            then(nc.vector.tensor_scalar(ebits, ebits, 1.0, None, ALU.is_lt))
            nc.vector.scalar_tensor_tensor(bad, own_max, 0.0, ebits, ALU.is_gt, ALU.max).then_inc(bad_ok, 1)

            def ending_in(k):
                kind, n = ENDS[k]
                t = end_tile(kind, n)
                if kind == "row":
                    bank = banks[n]
                else:
                    bank = COL_BANKS[n % 3]
                    I2, J, b = COLS[n]
                    dve.wait_ge(col_ps, n + 1)
                    dve.wait_ge(sums_ok, sums_written(I2, b))
                    nc.vector.tensor_tensor(sums(I2, b), bank[:, :], sums(I2, b), ALU.add).then_inc(col_end, 1)
                    dve.wait_ge(col_end, n - first_col + 1)
                    bank = sums(I2, b)
                if k >= 4:
                    dve.wait_ge(y_ok, k - 3)
                for v in range(2):
                    i = nc.vector.scalar_tensor_tensor(z_bufs[:, k % 4, v * C:(v + 1) * C], bank[:, v * C:(v + 1) * C],
                                                       down[:, t + v:t + v + 1], bias_rows[:, :], ALU.mult, ALU.add)
                i.then_inc(z_ok, 1)

            def ending_norm(k):
                t = end_tile(*ENDS[k])
                dve.wait_ge(z_ok, k + 1)
                zk = z_bufs[:, k % 4, :]
                nc.vector.scalar_tensor_tensor(zk, zk, SLOPE, zk, ALU.mult, ALU.max).then_inc(act_ok, 1)
                dve.wait_ge(act_ok, k + 1)
                nc.vector.tensor_tensor(zk, zk,
                                        x_late[:, t:t + 2, :].rearrange("p v n -> p (v n)"), ALU.add).then_inc(res_ok, 1)
                dve.wait_ge(res_ok, k + 1)
                for v in range(2):
                    i = nc.vector.bn_stats(stat(k, 6 * v, 6), z_bufs[:, k % 4, v * C:(v + 1) * C])
                then(i)
                for v in range(2):
                    i = nc.vector.bn_aggr(stat(k, 12 + 2 * v, 2), stat(k, 6 * v, 6))
                then(i)
                mv = stat(k, 12, 4).rearrange("p (v t) -> p v t", t=2)
                nc.vector.tensor_scalar(stat(k, 22, 2), mv[:, :, 0], -1.0, None, ALU.mult)
                nc.vector.tensor_scalar(stat(k, 16, 2), mv[:, :, 1], EPS, None, ALU.add).then_inc(var_ok, 1)

            dve.wait_ge(step_done, TILES)
            dve.wait_ge(w_ld, 48)
            ending_in(0)
            dve.wait_ge(xl_ld, 16 * SIDES * Q)
            for k in range(len(ENDS)):
                if k + 1 < len(ENDS):
                    ending_in(k + 1)
                ending_norm(k)
            dve.wait_ge(bad_all_ok, 1)
            nc.vector.tensor_copy(flag[:, :], bad_all).then_inc(flag_ok, 1)


def dense_path(nc, ctx, x, adj, wr, wd, bias, out):
    f32 = mybir.dt.float32
    ALU = mybir.AluOpType
    ACT = mybir.ActivationFunctionType
    AX = mybir.AxisListType

    def sb(name, shape):
        return ctx.enter_context(nc.sbuf_tensor("g_" + name, shape, f32))

    def pb(name, shape):
        return ctx.enter_context(nc.psum_tensor("g_" + name, shape, f32))

    def sem(name):
        return ctx.enter_context(nc.semaphore("g_" + name))

    adj_rows = [sb(f"adj_rows{u}", [P, N]) for u in range(2)]
    x_rows = [sb(f"x_rows{u}", [P, C]) for u in range(2)]
    x_cols = [sb(f"x_cols{u}", [P, KC * P]) for u in range(2)]
    adj_cols = [sb(f"adj_cols{u}", [P, GROUP * P]) for u in range(2)]
    weights = sb("weights", [P, 2, KC, C])
    feats = sb("feats", [P, TILES, C])
    bias_rows = sb("bias_rows", [P, C])
    ident = sb("ident", [P, P])
    deg = sb("deg", [P, 4])
    dinv = sb("dinv", [P, TILES])
    minus_half = sb("minus_half", [P, 1])
    z = sb("z", [P, 4, C])
    stats = sb("stats", [P, 16])
    y = [sb(f"y{u}", [P, C]) for u in range(2)]
    cols_ps = [pb(f"cols_ps{u}", [P, GROUP * P]) for u in range(2)]
    prod_ps = [pb(f"prod_ps{u}", [P, C]) for u in range(2)]

    const_ld = sem("const_ld")
    ident_ok = sem("ident_ok")
    a_ld = [sem(f"a_ld{u}") for u in range(2)]
    a_xT_ps = sem("a_xT_ps")
    a_xT = sem("a_xT")
    a_prod = sem("a_prod")
    a_deg = sem("a_deg")
    a_pow = sem("a_pow")
    a_feat = sem("a_feat")
    dve_step = sem("dve_step")
    b_ld = [sem(f"b_ld{u}") for u in range(2)]
    b_T_ps = sem("b_T_ps")
    b_T = sem("b_T")
    b_prod = sem("b_prod")
    b_read = sem("b_read")
    b_var = sem("b_var")
    b_rstd = sem("b_rstd")
    b_y = sem("b_y")
    b_st = [sem(f"b_st{u}") for u in range(2)]

    LINKS_A = 3
    LINKS_B = 6

    with nc.Block() as block:

        @block.sync
        def _(sp):
            for s, w in enumerate((wr, wd)):
                sp.dma_start(weights[:, s], w.rearrange("(k p) n -> p k n", p=P)).then_inc(const_ld, 16)
            sp.dma_start(bias_rows[:, :], bias.partition_broadcast(P)).then_inc(const_ld, 16)
            def load(rows, ld):
                for u, r in enumerate(rows):
                    sp.dma_start(x_rows[u][:, :], x[bass.ds(r * P, P), :]).then_inc(ld[u], 16)
                    sp.dma_start(adj_rows[u][:, :], adj[bass.ds(r * P, P), :]).then_inc(ld[u], 16)

            load((0, 1), a_ld)
            with sp.Fori(1, TILES // 2) as pair:
                i = pair * 2
                sp.wait_ge(a_feat, i)
                load((i, i + 1), a_ld)
            sp.wait_ge(a_feat, TILES)
            load((0, 1), b_ld)
            with sp.Fori(1, TILES // 2) as pair:
                i = pair * 2
                sp.wait_ge(b_read, i)
                load((i, i + 1), b_ld)

        @block.scalar
        def _(act):
            with act.Fori(0, TILES // 2) as pair:
                i = pair * 2
                for u in range(2):
                    act.wait_ge(a_xT_ps, i + u + 1)
                    nc.scalar.copy(x_cols[u][:, :], cols_ps[u][:, 0:KC * P]).then_inc(a_xT, 1)
            with act.Fori(0, TILES // 2) as pair:
                i = pair * 2
                for u in range(2):
                    for g in range(GROUPS):
                        act.wait_ge(b_T_ps, (i + u) * GROUPS + g + 1)
                        nc.scalar.copy(adj_cols[g % 2][:, :], cols_ps[g % 2][:, :]).then_inc(b_T, 1)

        @block.tensor
        def _(pe):
            pe.wait_ge(ident_ok, 3)
            pe.wait_ge(const_ld, 48)
            for s in range(2):
                with pe.Fori(s * HALF // 2, (s + 1) * HALF // 2) as pair:
                    i = pair * 2
                    for u in range(2):
                        pe.wait_ge(a_ld[u], i * 16 + 32)
                        for k in range(KC):
                            t = nc.tensor.transpose(cols_ps[u][:, k * P:(k + 1) * P],
                                                    x_rows[u][:, k * P:(k + 1) * P], ident[:, :])
                        t.then_inc(a_xT_ps, 1)
                        pe.wait_ge(a_xT, i + u + 1)
                        for k in range(KC):
                            m = nc.tensor.matmul(prod_ps[u][:, :], x_cols[u][:, k * P:(k + 1) * P],
                                                 weights[:, s, k, :], start=(k == 0), stop=(k == KC - 1))
                        m.then_inc(a_prod, 1)
            pe.wait_ge(a_feat, TILES)

            def transposes(u, g):
                for j in range(GROUP):
                    c = g * GROUP + j
                    t = nc.tensor.transpose(cols_ps[g % 2][:, j * P:(j + 1) * P],
                                            adj_rows[u][:, c * P:(c + 1) * P], ident[:, :])
                t.then_inc(b_T_ps, 1)

            with pe.Fori(0, TILES // 2) as pair:
                i = pair * 2
                for u in range(2):
                    pe.wait_ge(b_ld[u], i * 16 + 32)
                    transposes(u, 0)
                    for g in range(GROUPS):
                        if g + 1 < GROUPS:
                            transposes(u, g + 1)
                        pe.wait_ge(b_T, (i + u) * GROUPS + g + 1)
                        for j in range(GROUP):
                            c = g * GROUP + j
                            m = nc.tensor.matmul(prod_ps[u][:, :], adj_cols[g % 2][:, j * P:(j + 1) * P],
                                                 feats[:, c, :], start=(c == 0), stop=(c == TILES - 1))
                    m.then_inc(b_prod, 1)

        @block.gpsimd
        def _(pool):
            nc.gpsimd.memset(minus_half[:, :], -0.5).then_inc(ident_ok, 1)
            nc.gpsimd.memset(ident[:, :], 0.0).then_inc(ident_ok, 1)
            pool.wait_ge(ident_ok, 2)
            nc.gpsimd.affine_select(out=ident[:, :], in_=ident[:, :], compare_op=ALU.not_equal, fill=1.0, base=0,
                                    pattern=[[-1, P]], channel_multiplier=1).then_inc(ident_ok, 1)
            with pool.Fori(0, TILES // 2) as pair:
                i = pair * 2
                for u in range(2):
                    pool.wait_ge(a_deg, i + u + 1)
                    nc.gpsimd.tensor_tensor(deg[:, 2:3], deg[:, 1:2], minus_half[:, :], ALU.pow).then_inc(a_pow, 1)
            with pool.Fori(0, TILES // 2) as pair:
                i = pair * 2
                for u in range(2):
                    pool.wait_ge(b_var, i + u + 1)
                    nc.gpsimd.tensor_tensor(stats[:, 13:14], stats[:, 12:13], minus_half[:, :],
                                            ALU.pow).then_inc(b_rstd, 1)
                    pool.wait_ge(b_y, i + u + 1)
                    pool.dma_start(out[bass.ds((i + u) * P, P), :], y[u][:, :]).then_inc(b_st[u], 16)
                for u in range(2):
                    pool.wait_ge(b_st[u], i * 8 + 16)

        @block.vector
        def _(dve):
            with dve.Fori(0, TILES // 2) as pair:
                i = pair * 2
                for u in range(2):
                    t = i + u
                    links = [t * LINKS_A]

                    def link(ins):
                        ins.then_inc(dve_step, 1)
                        links[0] = links[0] + 1
                        dve.wait_ge(dve_step, links[0])

                    dve.wait_ge(a_ld[u], i * 16 + 32)
                    link(nc.vector.reduce_sum(deg[:, 0:1], adj_rows[u][:, :], axis=AX.X))
                    nc.vector.tensor_scalar(deg[:, 1:2], deg[:, 0:1], 1.0, 1e-38, ALU.add, ALU.max).then_inc(a_deg, 1)
                    link(nc.vector.tensor_scalar(deg[:, 3:4], deg[:, 0:1], 1.0, 0.0, ALU.add, ALU.is_gt))
                    dve.wait_ge(a_pow, t + 1)
                    link(nc.vector.tensor_tensor(dinv[:, bass.ds(t, 1)], deg[:, 2:3], deg[:, 3:4], ALU.mult))
                    dve.wait_ge(a_prod, t + 1)
                    nc.vector.tensor_scalar(feats[:, bass.ds(t, 1), :], prod_ps[u][:, :], dinv[:, bass.ds(t, 1)],
                                            None, ALU.mult).then_inc(a_feat, 1)
            dve.wait_ge(const_ld, 48)
            with dve.Fori(0, TILES // 2) as pair:
                i = pair * 2
                for u in range(2):
                    t = i + u
                    links = [t * LINKS_B + TILES * LINKS_A]

                    def link(ins):
                        ins.then_inc(dve_step, 1)
                        links[0] = links[0] + 1
                        dve.wait_ge(dve_step, links[0])

                    dve.wait_ge(b_prod, t + 1)
                    link(nc.vector.tensor_tensor(z[:, 0, :], prod_ps[u][:, :], feats[:, bass.ds(t, 1), :], ALU.add))
                    link(nc.vector.scalar_tensor_tensor(z[:, 1, :], z[:, 0, :], dinv[:, bass.ds(t, 1)],
                                                        bias_rows[:, :], ALU.mult, ALU.add))
                    link(nc.vector.scalar_tensor_tensor(z[:, 2, :], z[:, 1, :], SLOPE, z[:, 1, :], ALU.mult, ALU.max))
                    dve.wait_ge(b_ld[u], i * 16 + 32)
                    nc.vector.tensor_tensor(z[:, 3, :], z[:, 2, :], x_rows[u][:, :], ALU.add).then_inc(b_read, 1)
                    dve.wait_ge(b_read, t + 1)
                    link(nc.vector.bn_stats(stats[:, 0:6], z[:, 3, :]))
                    nc.vector.tensor_tensor(stats[:, 6:8], stats[:, 1:3], stats[:, 4:6], ALU.add)
                    link(nc.vector.tensor_tensor(stats[:, 8:9], stats[:, 1:2], stats[:, 4:5], ALU.subtract))
                    nc.vector.tensor_scalar(stats[:, 9:10], stats[:, 6:7], 0.5, None, ALU.mult)
                    nc.vector.tensor_scalar(stats[:, 11:12], stats[:, 7:8], 1.0 / C, EPS, ALU.mult, ALU.add)
                    link(nc.vector.tensor_tensor(stats[:, 10:11], stats[:, 8:9], stats[:, 8:9], ALU.mult))
                    nc.vector.scalar_tensor_tensor(stats[:, 12:13], stats[:, 10:11], 0.25, stats[:, 11:12],
                                                   ALU.mult, ALU.add).then_inc(b_var, 1)
                    dve.wait_ge(b_rstd, t + 1)
                    nc.vector.tensor_scalar(y[u][:, :], z[:, 3, :], stats[:, 9:10], stats[:, 13:14],
                                            ALU.subtract, ALU.mult).then_inc(b_y, 1)


def program(nc, x, adj, wr, wd, bias, out):
    with ExitStack() as ctx:
        flag = ctx.enter_context(nc.sbuf_tensor("flag", [P, 1], mybir.dt.int32))
        with ExitStack() as inner:
            split_path(nc, inner, x, adj, wr, wd, bias, out, flag)
        again = nc.values_load(flag[0:1, 0:1], min_val=0, max_val=1)
        with nc.If(again != 0):
            dense_path(nc, ctx, x, adj, wr, wd, bias, out)


_INS = ['x', 'adj', 'L0_gnn_weightr', 'L0_gnn_weightd', 'L0_gnn_bias']


def kernel(**inputs):
    import numpy as _np
    import concourse.bacc as _bacc
    from concourse import mybir as _mybir
    from concourse.bass_utils import run_bass_kernel_spmd as _run

    nc = _bacc.Bacc("TRN2", target_bir_lowering=False, num_devices=1)
    arrays, args = {}, []
    for name in _INS:
        a = _np.ascontiguousarray(inputs[name])
        arrays[f"in_{name}_dram"] = a
        args.append(nc.dram_tensor(f"in_{name}_dram", a.shape, _mybir.dt.from_np(a.dtype), kind="ExternalInput").ap())
    args.append(nc.dram_tensor("out_0_dram", (N, C), _mybir.dt.float32, kind="ExternalOutput").ap())
    program(nc, *args)
    r = _run(nc, [arrays], core_ids=[0])
    return r.results[0]["out_0_dram"]
```

```python
import concourse.bass as bass
from concourse import mybir
from contextlib import ExitStack

N = 4096
C = 256
P = 128
TILES = N // P
HALF = TILES // 2
KC = C // P
GROUP = 4
GROUPS = TILES // GROUP
SLOPE = 0.01
EPS = 1e-5

Q = 4
LANES = P // Q
SIDES = 2
PAIRS = HALF // 2
SB = 8
NSB = TILES // SB
UNIT = SB * P
PARTS = 2
BANK = 512
MANTISSA = 23
TOP = 10
F16_MAX = 65000.0
TOP_MIN = 16.0
DEG_MAX = float(N + 1)


def tile_rows(c):
    return c // HALF, c % HALF // 2, c % 2


def split_path(nc, ctx, x, adj, wr, wd, bias, out, flag):
    f32 = mybir.dt.float32
    f16 = mybir.dt.float16
    bf16 = mybir.dt.bfloat16
    u32 = mybir.dt.uint32
    i32 = mybir.dt.int32
    u16 = mybir.dt.uint16
    ALU = mybir.AluOpType
    ACT = mybir.ActivationFunctionType
    AX = mybir.AxisListType
    RMAX = bass.bass_isa.ReduceOp.max

    def sb(name, shape, dt=f32):
        return ctx.enter_context(nc.sbuf_tensor("s_" + name, shape, dt))

    def sem(name):
        return ctx.enter_context(nc.semaphore("s_" + name))

    feats = sb("feats", [P, TILES + 1, C])
    raw = sb("raw", [P, 4, 2 * N // Q])
    conv = sb("conv", [P, 2, 2, 2, N // Q], bf16)
    store = sb("store", [P, 62, UNIT], bf16)
    HELD = {(0, 1): 0, (2, 3): 0, (0, 3): 8, (0, 2): 16, (1, 2): 24, (1, 3): 32}
    DIAG = 40
    RING = {1: (48, 5), 2: (48, 3), 3: (16, 5)}
    SUMS = {0: 54, 1: 58, 2: 50}
    ident32 = store[:, 53, 0:2 * P].bitcast(f32)
    x_cols = store[:, 58:60, :].bitcast(f32)
    weights = store[:, 60:62, :].rearrange("p a b -> p (a b)").bitcast(f32).rearrange(
        "p (s k n) -> p s k n", s=2, k=KC)
    stats = store[:, 48, :].bitcast(f32)
    x_late = raw[:, :, :].rearrange("p a b -> p (a b)").rearrange("p (c n) -> p c n", n=C)
    z_bufs, y_bufs = (conv[:, h].rearrange("p a r w -> p (a r w)").bitcast(f32).rearrange("p (b n) -> p b n", b=4)
                      for h in range(2))

    GRANULES = TILES // 2 * Q
    X_UNITS = [24, 32, 26, 34, 28, 36, 30, 38]
    X_AFTER = {1: 1, 3: 2, 7: 3, 11: 4, 15: 5, 19: 6, 23: 7}
    LATE_ORDER = [NSB - 1] + list(range(NSB - 1))
    FIRST = 2
    EARLY = {pair: (2 * pair + 2, 2 * pair + 3) for pair in range(7)}

    LOOKERS = "adad"

    def looked_by(n, who):
        return LOOKERS[n % Q] == who

    bias_rows = sb("bias_rows", [P, C])
    same_lane = sb("same_lane", [P, P])
    ident16 = sb("ident16", [P, P], f16)
    row_parts = sb("row_parts", [P, 4, Q])
    own_quad = sb("own_quad", [P, Q])
    degs = sb("degs", [P, TILES])
    small = sb("small", [P, 26])
    good = sb("good", [P, TILES])
    dinv = sb("dinv", [P, TILES])
    up = sb("up", [P, 4])
    down = sb("down", [P, TILES])
    low_bits = sb("low_bits", [P, GRANULES])
    hmax = sb("hmax", [P, TILES // 2])
    own_max, gmax, unscale, ebits, bad, bad_all = (small[:, k:k + 1] for k in range(6))
    scales = small[:, 6:8]
    half_neg = small[:, 8:10]
    quad_sums = [small[:, 16 + r * Q:16 + (r + 1) * Q] for r in range(2)]

    banks = [ctx.enter_context(nc.psum_tensor(f"s_bank{k}", [P, BANK], f32)) for k in range(8)]
    COL_BANKS = banks[4:7]
    deg_bank = banks[7]

    w_ld = [sem(f"w_ld{k}") for k in range(2)]
    bias_ld = sem("bias_ld")
    x_ld = [sem(f"x_ld{k}") for k in range(2 * NSB)]
    xl_ld = [sem(f"xl_ld{I}") for I in range(NSB)]
    raw_ld = [sem(f"raw_ld{k}") for k in range(4)]
    consts = sem("consts")
    xT_ps, xT_ok = sem("xT_ps"), sem("xT_ok")
    h_ps, h_ok = sem("h_ps"), sem("h_ok")
    hmax_ok = sem("hmax_ok")
    gmax_ok = sem("gmax_ok")
    scale_ok = sem("scale_ok")
    conv_ok = sem("conv_ok")
    chk_act = sem("chk_act")
    chk_dve = sem("chk_dve")
    chk = {"a": chk_act, "d": chk_dve}
    turned = sem("turned")
    deg_ps = sem("deg_ps")
    deg_ok = sem("deg_ok")
    pow_ok = sem("pow_ok")
    up_ok = sem("up_ok")
    parts_ok = sem("parts_ok")
    rows_done = sem("rows_done")
    step_done = sem("step_done")
    rows_ok = sem("rows_ok")
    cols_ok = sem("cols_ok")
    col_ps = sem("col_ps")
    scaled_ok = sem("scaled_ok")
    link = sem("link")
    z_ok = sem("z_ok")
    leaky_ok = sem("leaky_ok")
    res_ok = sem("res_ok")
    var_ok = sem("var_ok")
    rstd_ok = sem("rstd_ok")
    shift_ok = sem("shift_ok")
    y_ok = sem("y_ok")
    stored = [sem(f"stored{k}") for k in range(4)]
    bad_ok = sem("bad_ok")
    bad_all_ok, flag_ok = sem("bad_all_ok"), sem("flag_ok")

    N_CONSTS = 3 + 2 * Q - 1

    def degs_cl(pair):
        return small[:, 10 + pair % 2 * 2:12 + pair % 2 * 2]

    def unit(c, J):
        I, e = divmod(c, SB)
        if J > I:
            return HELD[I, J] + e
        if J == I:
            return DIAG + e
        first, depth = RING[I]
        return first + e % depth * I + J

    def chunk(c, t):
        return store[:, unit(c, t // SB), :].rearrange("p (g m r) -> p g m r", m=P, r=2)[:, t % SB // 2, :, t % 2]

    def part(t, k):
        return feats[:, t, :].bitcast(f16)[:, k * C:(k + 1) * C]

    def sums(I, b):
        return store[:, SUMS[I] + b, :].bitcast(f32)

    def low(n, part=slice(None)):
        return raw[:, n % 4, part].bitcast(u16).rearrange("p (n t) -> p n t", t=2)[:, :, 0]

    def landed(n):
        return raw_ld[n % 4], 16 * Q * (n // 4 + 1)

    def looks(n):
        who = LOOKERS[n % Q]
        return chk[who], sum(looked_by(m, who) for m in range(n + 1))

    def x_early(b):
        return store[:, X_UNITS[b // 2] + b % 2, :].bitcast(f32)

    def products(b):
        return feats[:, 2 * b + 1:2 * b + 3, :].rearrange("p v n -> p (v n)")

    def stat(k, n, m=1):
        return stats[:, k % 4 * 24 + n:k % 4 * 24 + n + m]

    COLS = [(I, J, b) for J in range(1, NSB) for I in range(J) for b in range(SB // 2)]
    LAST = NSB - 1
    before = {n: max((m for m in range(n) if COLS[m][0] == COLS[n][0] and COLS[m][2] == COLS[n][2]), default=None)
              for n in range(len(COLS))}

    def rows_taken(I, b):
        return I * (SB // 2) + b + 1

    ENDS = [("row", b) for b in range(SB // 2)]
    for k, (I, J, b) in enumerate(COLS):
        if J == LAST:
            ENDS.append(("col", k))
    ENDS = [ENDS[k] for k in (0, 1, 4, 2, 5, 3)] + ENDS[6:]

    def end_tile(kind, k):
        return LAST * SB + 2 * k if kind == "row" else COLS[k][0] * SB + 2 * COLS[k][2]

    with nc.Block() as block:

        @block.sync
        def _(sp):
            def load_w(s, w):
                sp.dma_start(weights[:, s], w.rearrange("(k p) n -> p k n", p=P)).then_inc(w_ld[s], 16)

            x_v = x.rearrange("(s q g j r) n -> s q j g (r n)", s=SIDES, q=Q, g=PAIRS, j=LANES, r=2)

            def load_x(dst, ld, g, m):
                for q in range(Q):
                    sp.dma_start(dst[q * LANES:(q + 1) * LANES],
                                 x_v[g // PAIRS, q, :, g % PAIRS:g % PAIRS + m]).then_inc(ld, 16)

            def load_early(k):
                load_x(store[:, X_UNITS[k]:X_UNITS[k] + 2, :].bitcast(f32), x_ld[k], 2 * k, 2)

            load_early(0)
            load_w(0, wr)
            adj_v = adj.rearrange("(s a g u r) (t q w) -> s g a q u (r t) w", s=SIDES, a=Q, g=PAIRS, u=LANES, r=2,
                                  t=SIDES, q=Q)
            for n in range(GRANULES):
                pair, a = divmod(n, Q)
                if n >= 4:
                    sp.wait_ge(conv_ok, n - 3)
                    sp.wait_ge(*looks(n - 4))
                for q in range(Q):
                    sp.dma_start(raw[q * LANES:(q + 1) * LANES, n % 4, :].rearrange("p (m w) -> p m w", m=2 * SIDES),
                                 adj_v[pair // PAIRS, pair % PAIRS, a, q]).then_inc(raw_ld[n % 4], 16)
                if n in X_AFTER:
                    load_early(X_AFTER[n])
                if n == 6:
                    load_w(1, wd)
                    sp.dma_start(bias_rows[:, :], bias.partition_broadcast(P)).then_inc(bias_ld, 16)
            sp.wait_ge(conv_ok, GRANULES)
            for n in range(GRANULES - Q, GRANULES):
                sp.wait_ge(*looks(n))
            for I in LATE_ORDER:
                load_x(x_late[:, I * SB:(I + 1) * SB, :].rearrange("p (g r) n -> p g (r n)", r=2), xl_ld[I],
                       I * SB // 2, SB // 2)
            out_v = out.rearrange("(s q g j r) n -> s g q j (r n)", s=SIDES, q=Q, g=PAIRS, j=LANES, r=2)
            for k, end in enumerate(ENDS):
                s, g, _r = tile_rows(end_tile(*end))
                sp.wait_ge(y_ok, k + 1)
                for q in range(Q):
                    sp.dma_start(out_v[s, g, q], y_bufs[q * LANES:(q + 1) * LANES, k % 4, :]).then_inc(
                        stored[k % 4], 16)
            for k in range(4):
                sp.wait_ge(stored[k], 16 * Q * len(ENDS) // 4)

        @block.scalar
        def _(act):
            def look(n):
                act.wait_ge(conv_ok, n + 1)
                nc.scalar.activation(low(n), low(n), ACT.Copy, accum_out=low_bits[:, n:n + 1]).then_inc(chk_act, 1)

            TAKE_ROWS = {Q * ((I + 1) * SB // 2 + 1): I for I in range(LAST)}

            for n in range(GRANULES):
                pair, a = divmod(n, Q)
                if n in TAKE_ROWS:
                    I = TAKE_ROWS[n]
                    act.wait_ge(step_done, (I + 1) * SB)
                    if I == 1:
                        act.wait_ge(h_ps, 2 * PAIRS)
                    for b in range(SB // 2):
                        nc.scalar.copy(sums(I, b), banks[b][:, :]).then_inc(rows_ok, 1)
                act.wait_ge(*landed(n))
                if n % 2 == 0 and n >= 4:
                    act.wait_ge(turned, n // 2 - 1)
                if a == 0 and pair >= 2:
                    act.wait_ge(deg_ps, pair - 1)
                for r in range(2):
                    i = nc.scalar.activation(conv[:, n // 2 % 2, a % 2, r, :],
                                             raw[:, n % 4, r * N // Q:(r + 1) * N // Q], ACT.Copy,
                                             accum_out=row_parts[:, (2 * pair + r) % 4, a:a + 1])
                i.then_inc(conv_ok, 1)
                if n >= 1 and looked_by(n - 1, "a"):
                    look(n - 1)
            if looked_by(GRANULES - 1, "a"):
                look(GRANULES - 1)

            def finish(k):
                act.wait_ge(shift_ok, k + 1)
                for v in range(2):
                    i = nc.scalar.activation(y_bufs[:, k % 4, v * C:(v + 1) * C], z_bufs[:, k % 4, v * C:(v + 1) * C],
                                             ACT.Identity, bias=stat(k, 20 + v), scale=stat(k, 18 + v))
                i.then_inc(y_ok, 1)

            for k in range(len(ENDS)):
                if k >= 4:
                    act.wait_ge(stored[k % 4], 16 * Q * (k // 4))
                finish(k)

        @block.tensor
        def _(pe):
            def turn_x(b):
                if b % 2 == 0:
                    pe.wait_ge(x_ld[b // 2], 16 * Q)
                if b >= 2:
                    pe.wait_ge(xT_ok, b - 1)
                for v in range(2):
                    for k in range(KC):
                        i = nc.tensor.transpose(banks[4 + b % 2][:, (v * KC + k) * P:(v * KC + k + 1) * P],
                                                x_early(b)[:, (v * KC + k) * P:(v * KC + k + 1) * P], ident32)
                i.then_inc(xT_ps, 1)

            def make_features(b):
                pe.wait_ge(w_ld[b // (HALF // 2)], 16)
                pe.wait_ge(xT_ok, b + 1)
                if b >= 1:
                    pe.wait_ge(h_ok, b)
                for v in range(2):
                    for k in range(KC):
                        i = nc.tensor.matmul(banks[6][:, v * C:(v + 1) * C],
                                             x_cols[:, b % 2, (v * KC + k) * P:(v * KC + k + 1) * P],
                                             weights[:, b // (HALF // 2), k, :], start=(k == 0), stop=(k == KC - 1))
                i.then_inc(h_ps, 1)

            pe.wait_ge(consts, 2)
            turn_x(0)
            for b in range(FIRST):
                if b + 1 < FIRST:
                    turn_x(b + 1)
                make_features(b)

            pe.wait_ge(consts, N_CONSTS)
            for b in EARLY[0]:
                turn_x(b)

            def multiply_columns(k, tiles):
                I, J, b = COLS[k]
                for v in range(2):
                    row = I * SB + 2 * b + v
                    for t in tiles:
                        for m in range(PARTS):
                            i = nc.tensor.matmul(COL_BANKS[k % 3][:, v * C:(v + 1) * C], chunk(row, t), part(t, m),
                                                 start=(v == 0 and t == J * SB and m == 0),
                                                 stop=(t == (J + 1) * SB - 1 and m == PARTS - 1),
                                                 skip_group_check=True)
                return i

            BEGIN = {SB - 1: (0, 1, 2), SB + 1: (4, 5, 6)}
            begun = {k: 2 * pair for pair, ks in BEGIN.items() for k in ks}
            k_col = 0
            for pair in range(TILES // 2):
                pair_tiles = (2 * pair, 2 * pair + 1)
                I, e = divmod(2 * pair, SB)
                early = EARLY.get(pair)
                if early:
                    make_features(early[0])
                pe.wait_ge(conv_ok, Q * (pair + 1))
                if pair >= 1:
                    pe.wait_ge(deg_ok, pair)
                nc.tensor.matmul(deg_bank[:, pair * 2 * Q:(pair + 1) * 2 * Q], same_lane[:, :],
                                 row_parts[:, 2 * pair % 4:2 * pair % 4 + 2, :].rearrange("p c q -> p (c q)"),
                                 start=True, stop=True).then_inc(deg_ps, 1)
                if early:
                    make_features(early[1])
                for k in BEGIN.get(pair, ()):
                    if k < len(COL_BANKS):
                        pe.wait_ge(h_ok, 2 * PAIRS)
                    else:
                        pe.wait_ge(cols_ok, k - 2)
                    multiply_columns(k, range(I * SB, 2 * pair))
                opened = False

                def multiply(row, t, last):
                    nonlocal opened
                    for k in range(PARTS):
                        i = nc.tensor.matmul(banks[row % SB // 2][:, row % 2 * C:(row % 2 + 1) * C],
                                             chunk(row, t), part(t, k), start=row // 2 == pair and not opened,
                                             stop=last and k == PARTS - 1, skip_group_check=True)
                        opened = opened or row // 2 == pair
                    return i

                pe.wait_ge(turned, 2 * (pair + 1))
                if I >= 1:
                    pe.wait_ge(rows_ok, rows_taken(I - 1, e // 2))
                for row in pair_tiles:
                    for t in range(2 * pair):
                        i = multiply(row, t, False)
                    if pair >= SB // 2:
                        i.then_inc(rows_done, 1)
                for b in EARLY.get(pair + 1, ()):
                    turn_x(b)
                for c in pair_tiles:
                    pe.wait_ge(parts_ok, c + 1)
                    for row in pair_tiles:
                        multiply(row, c, False)
                    for k in range(PARTS):
                        i = nc.tensor.matmul(banks[e // 2][:, c % 2 * C:(c % 2 + 1) * C], ident16[:, :], part(c, k),
                                             start=False, stop=c % SB == SB - 1 and k == PARTS - 1,
                                             skip_group_check=True)
                    for row in range(I * SB, 2 * pair):
                        i = multiply(row, c, c % SB == SB - 1)
                    i.then_inc(step_done, 1)

                while c % SB == SB - 1 and k_col < len(COLS) and COLS[k_col][1] == I:
                    if k_col >= 3 and COLS[k_col - 3][1] < LAST:
                        pe.wait_ge(cols_ok, k_col - 2)
                    elif k_col >= 3:
                        pe.wait_ge(z_ok, ENDS.index(("col", k_col - 3)) + 1)
                    multiply_columns(k_col, range(begun.get(k_col, I * SB), (I + 1) * SB)).then_inc(col_ps, 1)
                    k_col += 1

        @block.gpsimd
        def _(pool):
            nc.gpsimd.memset(ident32, 0.0)
            nc.gpsimd.memset(ident16[:, :], 0.0)
            nc.gpsimd.memset(half_neg, -0.5)
            nc.gpsimd.memset(same_lane[:, :], 0.0).then_inc(consts, 1)
            diagonals = [(ident32, 0), (ident16[:, :], 0)] + [(same_lane[:, :], d) for d in range(LANES - P, P, LANES)]
            for n, (m, d) in enumerate(diagonals):
                pool.wait_ge(consts, n + 1)
                nc.gpsimd.affine_select(out=m, in_=m, compare_op=ALU.not_equal, fill=1.0, base=-d,
                                        pattern=[[-1, P]], channel_multiplier=1).then_inc(consts, 1)
            pool.wait_ge(hmax_ok, 1)
            nc.gpsimd.partition_all_reduce(gmax, own_max, P, RMAX).then_inc(gmax_ok, 1)
            for pair in range(TILES // 2):
                both = slice(2 * pair, 2 * pair + 2)
                pool.wait_ge(deg_ok, pair + 1)
                nc.gpsimd.tensor_tensor(dinv[:, both], degs_cl(pair), half_neg, ALU.pow).then_inc(pow_ok, 1)
                if pair == 0:
                    pool.wait_ge(scale_ok, 1)
                if pair >= 2:
                    pool.wait_ge(parts_ok, 2 * pair - 2)
                pool.wait_ge(pow_ok, pair + 1)
                nc.gpsimd.tensor_tensor(up[:, 2 * pair % 4:2 * pair % 4 + 2], dinv[:, both], scales,
                                        ALU.mult).then_inc(up_ok, 1)
            pool.wait_ge(bad_ok, 1)
            nc.gpsimd.partition_all_reduce(bad_all, bad, P, RMAX).then_inc(bad_all_ok, 1)

            def add_x(k):
                t = end_tile(*ENDS[k])
                pool.wait_ge(xl_ld[t // SB], 16 * Q)
                pool.wait_ge(leaky_ok, k + 1)
                zk = z_bufs[:, k % 4, :]
                nc.gpsimd.tensor_tensor(zk, zk, x_late[:, t:t + 2, :].rearrange("p v n -> p (v n)"),
                                        ALU.add).then_inc(res_ok, 1)

            add_x(0)
            for k in range(len(ENDS)):
                if k + 1 < len(ENDS):
                    add_x(k + 1)
                pool.wait_ge(var_ok, k + 1)
                nc.gpsimd.tensor_tensor(stat(k, 18, 2), stat(k, 16, 2), half_neg,
                                        ALU.pow).then_inc(rstd_ok, 1)
                pool.wait_ge(rstd_ok, k + 1)
                nc.gpsimd.tensor_tensor(stat(k, 20, 2), stat(k, 22, 2), stat(k, 18, 2), ALU.mult).then_inc(shift_ok, 1)

        @block.vector
        def _(dve):
            links = [0]

            def then(i):
                links[0] += 1
                i.then_inc(link, 1)
                dve.wait_ge(link, links[0])

            then(nc.vector.memset(own_quad[:, :], 0.0))
            for q in range(Q):
                i = nc.vector.memset(own_quad[q * LANES:(q + 1) * LANES, q:q + 1], 1.0)
            then(i)

            def turn_half(pair, h, cols):
                src = conv[:, h].rearrange("p a r w -> p (a r w)").bitcast(u32).rearrange(
                    "p (a r J m) -> p r J a m", a=2, r=2, J=NSB)
                for J in cols:
                    for c in (2 * pair, 2 * pair + 1):
                        I, e = divmod(c, SB)
                        if J < I and e >= RING[I][1]:
                            dve.wait_ge(rows_done, c - RING[I][1] + 1 - SB)
                        elif J < I and I == 2:
                            dve.wait_ge(rows_done, (I - 1) * SB)
                        elif J < I and I == LAST or J > I and I == 2:
                            dve.wait_ge(col_ps, ready_after(c) + 1)
                        elif J > I and I == 1:
                            dve.wait_ge(xT_ps, SB // 2 * (pair - SB // 2 + 1))
                        elif J == I and I >= 1:
                            dve.wait_ge(step_done, I * SB)
                        dst = store[:, unit(c, J), :].bitcast(u32).rearrange(
                            "p (g a u) -> p a g u", a=Q, u=LANES)[:, 2 * h:2 * h + 2]
                        i = nc.vector.transpose(dst, src[:, c % 2, J].rearrange("p a (g u) -> p a g u", u=LANES))
                return i

            head = {}

            def begin_half(pair, h):
                dve.wait_ge(conv_ok, Q * pair + 2 * h + 2)
                for n in (Q * pair + 2 * h, Q * pair + 2 * h + 1):
                    if looked_by(n, "d"):
                        look(n)

            def turn_head(pair, halves, cols):
                for h in halves:
                    begin_half(pair, h)
                    turn_half(pair, h, cols)
                    head[pair, h] = cols

            def turn(pair, after_first=None, before_second=None):
                for h in range(2):
                    if h == 1 and after_first:
                        after_first()
                    if (pair, h) not in head:
                        begin_half(pair, h)
                    if h == 1 and before_second:
                        before_second()
                    turn_half(pair, h, [J for J in range(NSB) if J not in head.get((pair, h), ())]).then_inc(turned, 1)

            def look(n):
                first, second = (low(n, slice(v * N // Q, (v + 1) * N // Q)) for v in range(2))
                nc.vector.tensor_tensor_reduce(out=first, in0=first, in1=second, scale=1.0, scalar=0.0, op0=ALU.add,
                                               op1=ALU.max, accum_out=low_bits[:, n:n + 1]).then_inc(chk_dve, 1)

            def ready_after(c):
                I, e = divmod(c, SB)
                return {2: e // 2, 3: SB // 2 + (e * I + I - 1) // 2}[I]

            def degrees(pair):
                dve.wait_ge(deg_ps, pair + 1)
                for r in range(2):
                    c = 2 * pair + r
                    i = nc.vector.tensor_tensor_reduce(out=quad_sums[r], in0=deg_bank[:, c * Q:(c + 1) * Q],
                                                       in1=own_quad[:, :], scale=1.0, scalar=1.0, op0=ALU.mult,
                                                       op1=ALU.add, accum_out=degs[:, c:c + 1])
                then(i)
                if pair >= 2:
                    dve.wait_ge(up_ok, pair - 1)
                nc.vector.tensor_scalar(degs_cl(pair), degs[:, 2 * pair:2 * pair + 2], 1.0, None,
                                        ALU.max).then_inc(deg_ok, 1)

            def make_parts(c):
                dve.wait_ge(up_ok, c // 2 + 1)
                if c % 2 == 1:
                    dve.wait_ge(parts_ok, c)
                f = up[:, c % 4:c % 4 + 1]
                then(nc.vector.tensor_scalar(part(c, 0), feats[:, c + 1, :], f, None, ALU.mult))
                nc.vector.scalar_tensor_tensor(part(c, 1), feats[:, c + 1, :], f, part(c, 0), ALU.mult,
                                               ALU.subtract).then_inc(parts_ok, 1)

            def keep_turned(b):
                dve.wait_ge(xT_ps, b + 1)
                nc.vector.tensor_copy(x_cols[:, b % 2, :], banks[4 + b % 2][:, :]).then_inc(xT_ok, 1)

            def keep_product(b):
                dve.wait_ge(h_ps, b + 1)
                nc.vector.tensor_copy(products(b), banks[6][:, :]).then_inc(h_ok, 1)

            def largest(b):
                dve.wait_ge(h_ok, b + 1)
                return nc.vector.tensor_reduce(hmax[:, b:b + 1], feats[:, 2 * b + 1:2 * b + 3, :], AX.XY, ALU.max,
                                               apply_absolute_value=True)

            for b in range(FIRST):
                keep_turned(b)
            for b in range(FIRST):
                keep_product(b)
                i = largest(b)
            then(i)
            nc.vector.tensor_reduce(own_max, hmax[:, 0:FIRST], AX.X, ALU.max).then_inc(hmax_ok, 1)
            turned_to = 0
            AHEAD = {1: range(PAIRS, 3 * PAIRS // 2), 2: range(3 * PAIRS // 2, 2 * PAIRS)}
            dve.wait_ge(gmax_ok, 1)
            then(nc.vector.tensor_scalar(ebits, gmax, 2.0 ** -100, None, ALU.max))
            then(nc.vector.tensor_scalar(ebits.bitcast(i32), ebits.bitcast(i32), 0x7F800000, None, ALU.bitwise_and))
            nc.vector.tensor_scalar(unscale.bitcast(i32), ebits.bitcast(i32), float(-(TOP << MANTISSA)), None, ALU.add)
            for r in range(2):
                i = nc.vector.tensor_scalar(scales[:, r:r + 1].bitcast(i32), ebits.bitcast(i32), -1.0,
                                            float((254 + TOP) << MANTISSA), ALU.mult, ALU.add)
            i.then_inc(scale_ok, 1)

            def add_columns(n):
                I, J, b = COLS[n]
                dve.wait_ge(col_ps, n + 1)
                if before[n] is None:
                    dve.wait_ge(rows_ok, rows_taken(I, b))
                else:
                    dve.wait_ge(cols_ok, before[n] + 1)
                nc.vector.tensor_tensor(sums(I, b), COL_BANKS[n % 3][:, :], sums(I, b), ALU.add).then_inc(cols_ok, 1)

            def scale_sums(n):
                I, b = divmod(n, SB // 2)
                dve.wait_ge(bias_ld, 16)
                if I == LAST - 1:
                    dve.wait_ge(rows_ok, rows_taken(I, b))
                else:
                    dve.wait_ge(cols_ok, before[COLS.index((I, LAST, b))] + 1)
                for v in range(2):
                    t = I * SB + 2 * b + v
                    half = sums(I, b)[:, v * C:(v + 1) * C]
                    i = nc.vector.scalar_tensor_tensor(half, half, down[:, t:t + 1], bias_rows[:, :],
                                                       ALU.mult, ALU.add)
                i.then_inc(scaled_ok, 1)

            SCALE_SUMS = {12: (0, 1, 2, 3), 13: (4, 5, 6, 7), 14: (8, 9), 15: (10, 11)}

            for pair in range(TILES // 2):
                I, e = divmod(2 * pair, SB)
                if pair == 0:
                    for b in EARLY[pair]:
                        keep_turned(b)

                def mid():
                    degrees(pair)
                    if pair in EARLY:
                        keep_product(EARLY[pair][0])

                def keep_early():
                    for b in EARLY.get(pair, ()) if pair else ():
                        keep_turned(b)

                if turned_to <= pair:
                    turn(turned_to, after_first=keep_early, before_second=mid)
                    turned_to += 1
                else:
                    mid()
                for c in (2 * pair, 2 * pair + 1):
                    make_parts(c)
                if pair in EARLY:
                    keep_product(EARLY[pair][1])
                if FIRST <= pair + 1 < PAIRS:
                    largest(pair + 1)
                for b in SCALE_SUMS.get(pair, ()):
                    scale_sums(b)
                if I >= 2 and turned_to < (I + 1) * SB // 2 and turned_to == pair + 1:
                    turn(turned_to)
                    turned_to += 1
                if e < SB - 2:
                    continue
                down_I = slice(I * SB, (I + 1) * SB)
                then(nc.vector.tensor_scalar(down[:, down_I], dinv[:, down_I], unscale, None, ALU.mult))
                if I == LAST:
                    break
                if I == 0:
                    turn_head(turned_to, (0,), (0, 2, 3))
                else:
                    for b in AHEAD[I]:
                        largest(b)
                    if I == 1:
                        turn_head(turned_to, (0, 1), (0, 1))
                for n in range(len(COLS)):
                    if COLS[n][1] == I:
                        add_columns(n)
                        nxt = 2 * turned_to + 1
                        if nxt - c - 1 < RING[I + 1][1] and ready_after(nxt) <= n:
                            turn(turned_to)
                            turned_to += 1

            for n in range(GRANULES - Q, GRANULES):
                dve.wait_ge(*looks(n))
            nc.vector.tensor_reduce(own_max, low_bits[:, :], AX.X, ALU.max)
            then(nc.vector.tensor_scalar(good[:, :], degs[:, :], 1.0, None, ALU.is_ge))
            then(nc.vector.scalar_tensor_tensor(good[:, :], degs[:, :], DEG_MAX, good[:, :], ALU.is_le, ALU.mult))
            then(nc.vector.tensor_reduce(ebits, good[:, :], AX.X, ALU.min))
            then(nc.vector.tensor_scalar(ebits, ebits, 1.0, None, ALU.is_lt))
            then(nc.vector.scalar_tensor_tensor(bad, own_max, 0.0, ebits, ALU.is_gt, ALU.max))
            then(nc.vector.tensor_reduce(own_max, hmax[:, :], AX.X, ALU.max))
            then(nc.vector.tensor_scalar(ebits, own_max, scales[:, 0:1], F16_MAX, ALU.mult, ALU.is_gt))
            then(nc.vector.tensor_tensor(bad, bad, ebits, ALU.max))
            then(nc.vector.tensor_reduce(own_max, hmax[:, :], AX.X, ALU.min))
            then(nc.vector.tensor_scalar(ebits, own_max, scales[:, 0:1], TOP_MIN, ALU.mult, ALU.is_lt))
            nc.vector.tensor_tensor(bad, bad, ebits, ALU.max).then_inc(bad_ok, 1)

            def ending_in(k):
                kind, n = ENDS[k]
                t = end_tile(kind, n)
                if kind == "col":
                    dve.wait_ge(col_ps, n + 1)
                if k >= 4:
                    dve.wait_ge(y_ok, k - 3)
                for v in range(2):
                    half = slice(v * C, (v + 1) * C)
                    if kind == "row":
                        bank, rest = banks[n][:, half], bias_rows[:, :]
                    else:
                        bank, rest = COL_BANKS[n % 3][:, half], sums(COLS[n][0], COLS[n][2])[:, half]
                    i = nc.vector.scalar_tensor_tensor(z_bufs[:, k % 4, half], bank, down[:, t + v:t + v + 1], rest,
                                                       ALU.mult, ALU.add)
                i.then_inc(z_ok, 1)
                dve.wait_ge(z_ok, k + 1)
                zk = z_bufs[:, k % 4, :]
                nc.vector.scalar_tensor_tensor(zk, zk, SLOPE, zk, ALU.mult, ALU.max).then_inc(leaky_ok, 1)

            def ending_norm(k):
                dve.wait_ge(res_ok, k + 1)
                for v in range(2):
                    i = nc.vector.bn_stats(stat(k, 6 * v, 6), z_bufs[:, k % 4, v * C:(v + 1) * C])
                then(i)
                for v in range(2):
                    i = nc.vector.bn_aggr(stat(k, 12 + 2 * v, 2), stat(k, 6 * v, 6))
                then(i)
                mv = stat(k, 12, 4).rearrange("p (v t) -> p v t", t=2)
                nc.vector.tensor_scalar(stat(k, 22, 2), mv[:, :, 0], -1.0, None, ALU.mult)
                nc.vector.tensor_scalar(stat(k, 16, 2), mv[:, :, 1], EPS, None, ALU.add).then_inc(var_ok, 1)

            dve.wait_ge(step_done, TILES)
            dve.wait_ge(scaled_ok, LAST * SB // 2)
            ending_in(0)
            for k in range(len(ENDS)):
                late = k >= len(ENDS) - 3
                if late:
                    ending_norm(k)
                if k + 1 < len(ENDS):
                    ending_in(k + 1)
                if not late:
                    ending_norm(k)
            dve.wait_ge(bad_all_ok, 1)
            nc.vector.tensor_copy(flag[:, :], bad_all).then_inc(flag_ok, 1)


def dense_path(nc, ctx, x, adj, wr, wd, bias, out):
    f32 = mybir.dt.float32
    ALU = mybir.AluOpType
    ACT = mybir.ActivationFunctionType
    AX = mybir.AxisListType

    def sb(name, shape):
        return ctx.enter_context(nc.sbuf_tensor("g_" + name, shape, f32))

    def pb(name, shape):
        return ctx.enter_context(nc.psum_tensor("g_" + name, shape, f32))

    def sem(name):
        return ctx.enter_context(nc.semaphore("g_" + name))

    adj_rows = [sb(f"adj_rows{u}", [P, N]) for u in range(2)]
    x_rows = [sb(f"x_rows{u}", [P, C]) for u in range(2)]
    x_cols = [sb(f"x_cols{u}", [P, KC * P]) for u in range(2)]
    adj_cols = [sb(f"adj_cols{u}", [P, GROUP * P]) for u in range(2)]
    weights = sb("weights", [P, 2, KC, C])
    feats = sb("feats", [P, TILES, C])
    bias_rows = sb("bias_rows", [P, C])
    ident = sb("ident", [P, P])
    deg = sb("deg", [P, 4])
    dinv = sb("dinv", [P, TILES])
    minus_half = sb("minus_half", [P, 1])
    z = sb("z", [P, 4, C])
    stats = sb("stats", [P, 16])
    y = [sb(f"y{u}", [P, C]) for u in range(2)]
    cols_ps = [pb(f"cols_ps{u}", [P, GROUP * P]) for u in range(2)]
    prod_ps = [pb(f"prod_ps{u}", [P, C]) for u in range(2)]

    const_ld = sem("const_ld")
    ident_ok = sem("ident_ok")
    a_ld = [sem(f"a_ld{u}") for u in range(2)]
    a_xT_ps = sem("a_xT_ps")
    a_xT = sem("a_xT")
    a_prod = sem("a_prod")
    a_deg = sem("a_deg")
    a_pow = sem("a_pow")
    a_feat = sem("a_feat")
    dve_step = sem("dve_step")
    b_ld = [sem(f"b_ld{u}") for u in range(2)]
    b_T_ps = sem("b_T_ps")
    b_T = sem("b_T")
    b_prod = sem("b_prod")
    b_read = sem("b_read")
    b_var = sem("b_var")
    b_rstd = sem("b_rstd")
    b_y = sem("b_y")
    b_st = [sem(f"b_st{u}") for u in range(2)]

    LINKS_A = 3
    LINKS_B = 6

    with nc.Block() as block:

        @block.sync
        def _(sp):
            for s, w in enumerate((wr, wd)):
                sp.dma_start(weights[:, s], w.rearrange("(k p) n -> p k n", p=P)).then_inc(const_ld, 16)
            sp.dma_start(bias_rows[:, :], bias.partition_broadcast(P)).then_inc(const_ld, 16)
            def load(rows, ld):
                for u, r in enumerate(rows):
                    sp.dma_start(x_rows[u][:, :], x[bass.ds(r * P, P), :]).then_inc(ld[u], 16)
                    sp.dma_start(adj_rows[u][:, :], adj[bass.ds(r * P, P), :]).then_inc(ld[u], 16)

            load((0, 1), a_ld)
            with sp.Fori(1, TILES // 2) as pair:
                i = pair * 2
                sp.wait_ge(a_feat, i)
                load((i, i + 1), a_ld)
            sp.wait_ge(a_feat, TILES)
            load((0, 1), b_ld)
            with sp.Fori(1, TILES // 2) as pair:
                i = pair * 2
                sp.wait_ge(b_read, i)
                load((i, i + 1), b_ld)

        @block.scalar
        def _(act):
            with act.Fori(0, TILES // 2) as pair:
                i = pair * 2
                for u in range(2):
                    act.wait_ge(a_xT_ps, i + u + 1)
                    nc.scalar.copy(x_cols[u][:, :], cols_ps[u][:, 0:KC * P]).then_inc(a_xT, 1)
            with act.Fori(0, TILES // 2) as pair:
                i = pair * 2
                for u in range(2):
                    for g in range(GROUPS):
                        act.wait_ge(b_T_ps, (i + u) * GROUPS + g + 1)
                        nc.scalar.copy(adj_cols[g % 2][:, :], cols_ps[g % 2][:, :]).then_inc(b_T, 1)

        @block.tensor
        def _(pe):
            pe.wait_ge(ident_ok, 3)
            pe.wait_ge(const_ld, 48)
            for s in range(2):
                with pe.Fori(s * HALF // 2, (s + 1) * HALF // 2) as pair:
                    i = pair * 2
                    for u in range(2):
                        pe.wait_ge(a_ld[u], i * 16 + 32)
                        for k in range(KC):
                            t = nc.tensor.transpose(cols_ps[u][:, k * P:(k + 1) * P],
                                                    x_rows[u][:, k * P:(k + 1) * P], ident[:, :])
                        t.then_inc(a_xT_ps, 1)
                        pe.wait_ge(a_xT, i + u + 1)
                        for k in range(KC):
                            m = nc.tensor.matmul(prod_ps[u][:, :], x_cols[u][:, k * P:(k + 1) * P],
                                                 weights[:, s, k, :], start=(k == 0), stop=(k == KC - 1))
                        m.then_inc(a_prod, 1)
            pe.wait_ge(a_feat, TILES)

            def transposes(u, g):
                for j in range(GROUP):
                    c = g * GROUP + j
                    t = nc.tensor.transpose(cols_ps[g % 2][:, j * P:(j + 1) * P],
                                            adj_rows[u][:, c * P:(c + 1) * P], ident[:, :])
                t.then_inc(b_T_ps, 1)

            with pe.Fori(0, TILES // 2) as pair:
                i = pair * 2
                for u in range(2):
                    pe.wait_ge(b_ld[u], i * 16 + 32)
                    transposes(u, 0)
                    for g in range(GROUPS):
                        if g + 1 < GROUPS:
                            transposes(u, g + 1)
                        pe.wait_ge(b_T, (i + u) * GROUPS + g + 1)
                        for j in range(GROUP):
                            c = g * GROUP + j
                            m = nc.tensor.matmul(prod_ps[u][:, :], adj_cols[g % 2][:, j * P:(j + 1) * P],
                                                 feats[:, c, :], start=(c == 0), stop=(c == TILES - 1))
                    m.then_inc(b_prod, 1)

        @block.gpsimd
        def _(pool):
            nc.gpsimd.memset(minus_half[:, :], -0.5).then_inc(ident_ok, 1)
            nc.gpsimd.memset(ident[:, :], 0.0).then_inc(ident_ok, 1)
            pool.wait_ge(ident_ok, 2)
            nc.gpsimd.affine_select(out=ident[:, :], in_=ident[:, :], compare_op=ALU.not_equal, fill=1.0, base=0,
                                    pattern=[[-1, P]], channel_multiplier=1).then_inc(ident_ok, 1)
            with pool.Fori(0, TILES // 2) as pair:
                i = pair * 2
                for u in range(2):
                    pool.wait_ge(a_deg, i + u + 1)
                    nc.gpsimd.tensor_tensor(deg[:, 2:3], deg[:, 1:2], minus_half[:, :], ALU.pow).then_inc(a_pow, 1)
            with pool.Fori(0, TILES // 2) as pair:
                i = pair * 2
                for u in range(2):
                    pool.wait_ge(b_var, i + u + 1)
                    nc.gpsimd.tensor_tensor(stats[:, 13:14], stats[:, 12:13], minus_half[:, :],
                                            ALU.pow).then_inc(b_rstd, 1)
                    pool.wait_ge(b_y, i + u + 1)
                    pool.dma_start(out[bass.ds((i + u) * P, P), :], y[u][:, :]).then_inc(b_st[u], 16)
                for u in range(2):
                    pool.wait_ge(b_st[u], i * 8 + 16)

        @block.vector
        def _(dve):
            with dve.Fori(0, TILES // 2) as pair:
                i = pair * 2
                for u in range(2):
                    t = i + u
                    links = [t * LINKS_A]

                    def link(ins):
                        ins.then_inc(dve_step, 1)
                        links[0] = links[0] + 1
                        dve.wait_ge(dve_step, links[0])

                    dve.wait_ge(a_ld[u], i * 16 + 32)
                    link(nc.vector.reduce_sum(deg[:, 0:1], adj_rows[u][:, :], axis=AX.X))
                    nc.vector.tensor_scalar(deg[:, 1:2], deg[:, 0:1], 1.0, 1e-38, ALU.add, ALU.max).then_inc(a_deg, 1)
                    link(nc.vector.tensor_scalar(deg[:, 3:4], deg[:, 0:1], 1.0, 0.0, ALU.add, ALU.is_gt))
                    dve.wait_ge(a_pow, t + 1)
                    link(nc.vector.tensor_tensor(dinv[:, bass.ds(t, 1)], deg[:, 2:3], deg[:, 3:4], ALU.mult))
                    dve.wait_ge(a_prod, t + 1)
                    nc.vector.tensor_scalar(feats[:, bass.ds(t, 1), :], prod_ps[u][:, :], dinv[:, bass.ds(t, 1)],
                                            None, ALU.mult).then_inc(a_feat, 1)
            dve.wait_ge(const_ld, 48)
            with dve.Fori(0, TILES // 2) as pair:
                i = pair * 2
                for u in range(2):
                    t = i + u
                    links = [t * LINKS_B + TILES * LINKS_A]

                    def link(ins):
                        ins.then_inc(dve_step, 1)
                        links[0] = links[0] + 1
                        dve.wait_ge(dve_step, links[0])

                    dve.wait_ge(b_prod, t + 1)
                    link(nc.vector.tensor_tensor(z[:, 0, :], prod_ps[u][:, :], feats[:, bass.ds(t, 1), :], ALU.add))
                    link(nc.vector.scalar_tensor_tensor(z[:, 1, :], z[:, 0, :], dinv[:, bass.ds(t, 1)],
                                                        bias_rows[:, :], ALU.mult, ALU.add))
                    link(nc.vector.scalar_tensor_tensor(z[:, 2, :], z[:, 1, :], SLOPE, z[:, 1, :], ALU.mult, ALU.max))
                    dve.wait_ge(b_ld[u], i * 16 + 32)
                    nc.vector.tensor_tensor(z[:, 3, :], z[:, 2, :], x_rows[u][:, :], ALU.add).then_inc(b_read, 1)
                    dve.wait_ge(b_read, t + 1)
                    link(nc.vector.bn_stats(stats[:, 0:6], z[:, 3, :]))
                    nc.vector.tensor_tensor(stats[:, 6:8], stats[:, 1:3], stats[:, 4:6], ALU.add)
                    link(nc.vector.tensor_tensor(stats[:, 8:9], stats[:, 1:2], stats[:, 4:5], ALU.subtract))
                    nc.vector.tensor_scalar(stats[:, 9:10], stats[:, 6:7], 0.5, None, ALU.mult)
                    nc.vector.tensor_scalar(stats[:, 11:12], stats[:, 7:8], 1.0 / C, EPS, ALU.mult, ALU.add)
                    link(nc.vector.tensor_tensor(stats[:, 10:11], stats[:, 8:9], stats[:, 8:9], ALU.mult))
                    nc.vector.scalar_tensor_tensor(stats[:, 12:13], stats[:, 10:11], 0.25, stats[:, 11:12],
                                                   ALU.mult, ALU.add).then_inc(b_var, 1)
                    dve.wait_ge(b_rstd, t + 1)
                    nc.vector.tensor_scalar(y[u][:, :], z[:, 3, :], stats[:, 9:10], stats[:, 13:14],
                                            ALU.subtract, ALU.mult).then_inc(b_y, 1)


def program(nc, x, adj, wr, wd, bias, out):
    with ExitStack() as ctx:
        flag = ctx.enter_context(nc.sbuf_tensor("flag", [P, 1], mybir.dt.int32))
        with ExitStack() as inner:
            split_path(nc, inner, x, adj, wr, wd, bias, out, flag)
        again = nc.values_load(flag[0:1, 0:1], min_val=0, max_val=1)
        with nc.If(again != 0):
            dense_path(nc, ctx, x, adj, wr, wd, bias, out)


_INS = ['x', 'adj', 'L0_gnn_weightr', 'L0_gnn_weightd', 'L0_gnn_bias']


def kernel(**inputs):
    import numpy as _np
    import concourse.bacc as _bacc
    from concourse import mybir as _mybir
    from concourse.bass_utils import run_bass_kernel_spmd as _run

    nc = _bacc.Bacc("TRN2", target_bir_lowering=False, num_devices=1)
    arrays, args = {}, []
    for name in _INS:
        a = _np.ascontiguousarray(inputs[name])
        arrays[f"in_{name}_dram"] = a
        args.append(nc.dram_tensor(f"in_{name}_dram", a.shape, _mybir.dt.from_np(a.dtype), kind="ExternalInput").ap())
    args.append(nc.dram_tensor("out_0_dram", (N, C), _mybir.dt.float32, kind="ExternalOutput").ap())
    program(nc, *args)
    r = _run(nc, [arrays], core_ids=[0])
    return r.results[0]["out_0_dram"]
```
